# Optimizing a Trainium2 kernel written in Bass

```python
import numpy as np
import jax
import jax.numpy as jnp

def _softmax(x, axis=-1):
    return jax.nn.softmax(x, axis=axis)

def _gelu(x):
    return jax.nn.gelu(x, approximate=True)

def _silu(x):
    return jax.nn.silu(x)

def _sigmoid(x):
    return jax.nn.sigmoid(x)

def _layernorm(x, axis=-1, eps=1e-05):
    m = jnp.mean(x, axis=axis, keepdims=True)
    v = jnp.var(x, axis=axis, keepdims=True)
    return (x - m) / jnp.sqrt(v + eps)

def _scatter_add(tgt, idx, src, axis=0):
    return tgt.at[idx].add(src)

def _segment_sum(src, seg, n):
    return jax.ops.segment_sum(src, seg, n)
kernel_name = 'mk_seq_postln_d2_jaxref_r8_0cbe8a'

def setup_inputs(seed: int=0):
    np.random.seed(seed)
    _w = jnp.asarray

    def _L0_attn_setup():
        import jax, jax.numpy as jnp
        import numpy as np
        DIM = 128
        H = 16
        D = DIM // H
        HID = H * D
        N, T = (2, 128)
        key = jax.random.key(seed)
        ks = jax.random.split(key, 6)
        x = jax.random.normal(ks[0], (N, T, DIM), dtype=jnp.float32)
        key_w = jax.random.normal(ks[1], (HID, DIM), dtype=jnp.float32) * DIM ** (-0.5)
        key_b = jax.random.uniform(ks[2], (HID,), minval=-4.0, maxval=4.0, dtype=jnp.float32)
        vq_w = jax.random.normal(ks[3], (2 * HID, DIM), dtype=jnp.float32) * DIM ** (-0.5)
        out_w = jax.random.normal(ks[4], (DIM, HID), dtype=jnp.float32) * HID ** (-0.5)
        out_b = jax.random.normal(ks[5], (DIM,), dtype=jnp.float32) * 0.02
        return {'x': x, 'key_w': key_w, 'key_b': key_b, 'vq_w': vq_w, 'out_w': out_w, 'out_b': out_b}
    _L0_attn_in = _L0_attn_setup()

    def _L0_ffn_setup():
        import jax, jax.numpy as jnp
        import numpy as np
        NUM_OPS, B, T, D = (8, 8, 64, 128)
        key = jax.random.key(seed)
        k1, k2, k3, k4 = jax.random.split(key, 4)
        x = jax.random.normal(k1, (B, T, D), dtype=jnp.float32)
        W = jax.random.normal(k2, (NUM_OPS, D, D), dtype=jnp.float32) * 0.02
        b = jnp.zeros((NUM_OPS, D), dtype=jnp.float32)
        logits = 0.001 * jax.random.normal(k3, (NUM_OPS,), dtype=jnp.float32)
        u = jax.random.uniform(k4, (NUM_OPS,), dtype=jnp.float32, minval=1e-06, maxval=1.0 - 1e-06)
        return {'x': x, 'W': W, 'b': b, 'logits': logits, 'u': u}
    _L0_ffn_in = _L0_ffn_setup()

    def _L1_attn_setup():
        import jax, jax.numpy as jnp
        import numpy as np
        K_DIM = 64
        SQRT_K = float(np.sqrt(K_DIM))

        def build_metric(halves, diagonals_nk):
            H, K = diagonals_nk.shape
            iu, ju = np.triu_indices(K, k=1)
            m = jnp.zeros((H, K, K), dtype=halves.dtype).at[:, iu, ju].set(halves)
            m = m + m.transpose(0, 2, 1)
            d = np.arange(K)
            return m.at[:, d, d].set(diagonals_nk)
        key = jax.random.key(seed)
        ks = jax.random.split(key, 6)
        B, W, C, H = (2, 256, 128, 16)
        K = C // H
        return {'in_sequence_bwc': jax.random.normal(ks[0], (B, W, C), dtype=jnp.float32), 'projection_1nck': jax.random.normal(ks[1], (1, H, C, K), dtype=jnp.float32), 'halves': jax.random.normal(ks[2], (H, K * (K + 1) // 2 - K), dtype=jnp.float32), 'diagonals_nk': jax.random.normal(ks[3], (H, K), dtype=jnp.float32), 'mixer_w': jax.random.normal(ks[4], (C, C), dtype=jnp.float32), 'mixer_b': jax.random.normal(ks[5], (C,), dtype=jnp.float32)}
    _L1_attn_in = _L1_attn_setup()

    def _L1_ffn_setup():
        import jax, jax.numpy as jnp
        import numpy as np
        D_IN, D_HID = (128, 512)

        def _ternary(key, shape):
            return jax.random.randint(key, shape, -1, 2).astype(jnp.float32)

        def _tlin(x, w, s):
            return jnp.einsum('bsi,oi->bso', x, w) * s
        key = jax.random.key(seed)
        ks = jax.random.split(key, 12)
        inv = lambda fan: 1.0 / np.sqrt(fan).astype(np.float32)
        return {'x': jax.random.normal(ks[0], (4, 256, D_IN), dtype=jnp.float32), 'w1_w': _ternary(ks[1], (D_HID, D_IN)), 'w1_s': jax.random.uniform(ks[2], (D_HID,), dtype=jnp.float32) * inv(D_IN), 'w2_w': _ternary(ks[3], (D_HID, D_IN)), 'w2_s': jax.random.uniform(ks[4], (D_HID,), dtype=jnp.float32) * inv(D_IN), 'h1_w': _ternary(ks[5], (D_HID, D_HID)), 'h1_s': jax.random.uniform(ks[6], (D_HID,), dtype=jnp.float32) * inv(D_HID), 'h2_w': _ternary(ks[7], (D_HID, D_HID)), 'h2_s': jax.random.uniform(ks[8], (D_HID,), dtype=jnp.float32) * inv(D_HID), 'w3_w': _ternary(ks[9], (D_IN, D_HID)), 'w3_s': jax.random.uniform(ks[10], (D_IN,), dtype=jnp.float32) * inv(D_HID)}
    _L1_ffn_in = _L1_ffn_setup()
    _d = {'L0_attn_x': _L0_attn_in['x'], 'L0_attn_key_w': _L0_attn_in['key_w'], 'L0_attn_key_b': _L0_attn_in['key_b'], 'L0_attn_vq_w': _L0_attn_in['vq_w'], 'L0_attn_out_w': _L0_attn_in['out_w'], 'L0_attn_out_b': _L0_attn_in['out_b'], 'L0_ffn_W': _L0_ffn_in['W'], 'L0_ffn_b': _L0_ffn_in['b'], 'L0_ffn_logits': _L0_ffn_in['logits'], 'L0_ffn_u': _L0_ffn_in['u'], 'L1_attn_projection_1nck': _L1_attn_in['projection_1nck'], 'L1_attn_halves': _L1_attn_in['halves'], 'L1_attn_diagonals_nk': _L1_attn_in['diagonals_nk'], 'L1_attn_mixer_w': _L1_attn_in['mixer_w'], 'L1_attn_mixer_b': _L1_attn_in['mixer_b'], 'L1_ffn_w1_w': _L1_ffn_in['w1_w'], 'L1_ffn_w1_s': _L1_ffn_in['w1_s'], 'L1_ffn_w2_w': _L1_ffn_in['w2_w'], 'L1_ffn_w2_s': _L1_ffn_in['w2_s'], 'L1_ffn_h1_w': _L1_ffn_in['h1_w'], 'L1_ffn_h1_s': _L1_ffn_in['h1_s'], 'L1_ffn_h2_w': _L1_ffn_in['h2_w'], 'L1_ffn_h2_s': _L1_ffn_in['h2_s'], 'L1_ffn_w3_w': _L1_ffn_in['w3_w'], 'L1_ffn_w3_s': _L1_ffn_in['w3_s']}
    _x0 = _d['L0_attn_x']
    _d['L0_attn_x'] = jax.random.normal(jax.random.fold_in(jax.random.key(seed), 1), (8, 256, 128), dtype=_x0.dtype)
    del _x0
    return _d

def reference(L0_attn_x, L0_attn_key_w, L0_attn_key_b, L0_attn_vq_w, L0_attn_out_w, L0_attn_out_b, L0_ffn_W, L0_ffn_b, L0_ffn_logits, L0_ffn_u, L1_attn_projection_1nck, L1_attn_halves, L1_attn_diagonals_nk, L1_attn_mixer_w, L1_attn_mixer_b, L1_ffn_w1_w, L1_ffn_w1_s, L1_ffn_w2_w, L1_ffn_w2_s, L1_ffn_h1_w, L1_ffn_h1_s, L1_ffn_h2_w, L1_ffn_h2_s, L1_ffn_w3_w, L1_ffn_w3_s):

    def _L0_attn_ref(x, key_w, key_b, vq_w, out_w, out_b):
        import jax, jax.numpy as jnp
        import numpy as np
        DIM = 128
        H = 16
        D = DIM // H
        HID = H * D
        N, T = (2, 128)
        n, t, dim = x.shape
        vq = x @ vq_w.T
        v, q = jnp.split(vq, 2, axis=-1)
        k = jax.nn.sigmoid(x @ key_w.T + key_b)
        k = k.reshape(n, t, H, D)
        v = v.reshape(n, t, H, D)
        upd = (1.0 - k)[..., :, None] * v[..., None, :]
        decay = k[..., :, None]

        def combine(c1, c2):
            a1, b1 = c1
            a2, b2 = c2
            return (a1 * a2, b1 * a2 + b2)
        _, kv = jax.lax.associative_scan(combine, (decay, upd), axis=1)
        qh = q.reshape(n, t, H, D)
        h = jnp.einsum('nthd,nthde->nthe', qh, kv).reshape(n, t, HID)
        return h @ out_w.T + out_b

    def _L0_ffn_ref(x, W, b, logits, u):
        import jax, jax.numpy as jnp
        import numpy as np
        NUM_OPS, B, T, D = (8, 8, 64, 128)
        gumbel = -jnp.log(-jnp.log(u))
        idx = jnp.argmax(jax.nn.log_softmax(logits) + gumbel)
        out = jnp.einsum('btd,de->bte', x, W[idx]) + b[idx]
        return out

    def _L1_attn_ref(in_sequence_bwc, projection_1nck, halves, diagonals_nk, mixer_w, mixer_b):
        import jax, jax.numpy as jnp
        import numpy as np
        K_DIM = 64
        SQRT_K = float(np.sqrt(K_DIM))

        def build_metric(halves, diagonals_nk):
            H, K = diagonals_nk.shape
            iu, ju = np.triu_indices(K, k=1)
            m = jnp.zeros((H, K, K), dtype=halves.dtype).at[:, iu, ju].set(halves)
            m = m + m.transpose(0, 2, 1)
            d = np.arange(K)
            return m.at[:, d, d].set(diagonals_nk)
        B, W, C = in_sequence_bwc.shape
        metric_nkk = build_metric(halves, diagonals_nk)
        proj_nck = projection_1nck[0]
        proj_bnwk = jnp.einsum('bwc,nck->bnwk', in_sequence_bwc, proj_nck)
        pm_bnwk = jnp.einsum('bnwk,nkl->bnwl', proj_bnwk, metric_nkk)
        dots_bnww = jnp.einsum('bnwl,bnvl->bnwv', pm_bnwk, proj_bnwk)
        nudged_bnwk = jnp.einsum('bnwv,bnvk->bnwk', dots_bnww, proj_bnwk)
        nudged_bwc = nudged_bnwk.transpose(0, 2, 1, 3).reshape(B, W, C)
        return nudged_bwc @ mixer_w.T + mixer_b

    def _L1_ffn_ref(x, w1_w, w1_s, w2_w, w2_s, h1_w, h1_s, h2_w, h2_s, w3_w, w3_s):
        import jax, jax.numpy as jnp
        import numpy as np
        D_IN, D_HID = (128, 512)

        def _ternary(key, shape):
            return jax.random.randint(key, shape, -1, 2).astype(jnp.float32)

        def _tlin(x, w, s):
            return jnp.einsum('bsi,oi->bso', x, w) * s
        h = jax.nn.silu(_tlin(x, w1_w, w1_s)) * _tlin(x, w2_w, w2_s)
        h = jax.nn.gelu(_tlin(h, h1_w, h1_s), approximate=False)
        h = jax.nn.gelu(_tlin(h, h2_w, h2_s), approximate=False)
        return _tlin(h, w3_w, w3_s)
    x = L0_attn_x
    x = _layernorm(x + _L0_attn_ref(x, L0_attn_key_w, L0_attn_key_b, L0_attn_vq_w, L0_attn_out_w, L0_attn_out_b), axis=-1)
    x = _layernorm(x + _L0_ffn_ref(x, L0_ffn_W, L0_ffn_b, L0_ffn_logits, L0_ffn_u), axis=-1)
    x = _layernorm(x + _L1_attn_ref(x, L1_attn_projection_1nck, L1_attn_halves, L1_attn_diagonals_nk, L1_attn_mixer_w, L1_attn_mixer_b), axis=-1)
    x = _layernorm(x + _L1_ffn_ref(x, L1_ffn_w1_w, L1_ffn_w1_s, L1_ffn_w2_w, L1_ffn_w2_s, L1_ffn_h1_w, L1_ffn_h1_s, L1_ffn_h2_w, L1_ffn_h2_s, L1_ffn_w3_w, L1_ffn_w3_s), axis=-1)
    return x

_drawn_inputs = setup_inputs


def setup_inputs(seed=0):
    import zlib

    import numpy as np

    out = dict(_drawn_inputs(seed))
    spreads = {'L0_ffn_b': (0.0, 0.1)}
    factors = {'L0_attn_out_b': 3.736,
     'L1_attn_mixer_b': 8.0,
     'L1_ffn_w1_w': 8.0,
     'L1_ffn_w1_s': 8.0,
     'L1_ffn_w2_w': 8.0,
     'L1_ffn_w2_s': 8.0,
     'L1_ffn_h1_w': 8.0,
     'L1_ffn_h1_s': 8.0,
     'L1_ffn_h2_w': 8.0,
     'L1_ffn_h2_s': 8.0,
     'L1_ffn_w3_w': 8.0,
     'L1_ffn_w3_s': 8.0}
    for name, (base, spread) in spreads.items():
        noise = np.random.default_rng([zlib.crc32(name.encode()), seed]).standard_normal(out[name].shape)
        drawn = base * np.exp(spread * noise) if base else spread * noise
        out[name] = jnp.asarray(drawn.astype(out[name].dtype))
    for name, factor in factors.items():
        out[name] = (out[name] * factor).astype(out[name].dtype)
    return out
```

```python
from contextlib import ExitStack

import concourse.bass as bass
from concourse import mybir

F32 = mybir.dt.float32
ALU = mybir.AluOpType
ACT = mybir.ActivationFunctionType
AX_X = mybir.AxisListType.X

P = 128
SEQS, SEQ = 8, 256
GS = 2
T = GS * SEQ
NT = T // P
NG = SEQS // GS
TPS = SEQ // P
HEADS, HD = 16, 8
OPS = 8
HID = 512
NH = HID // P
EPS = 1e-5
STATES = 4
CREDIT = 1

PJ, RP, B4, B5, C6, C7 = 4, HD, 5, 4, 2 * NH + 1, 2 * NH


def nth(group, per_group, k):
    return group * per_group + k


PACKS = (
    ("project", (("key_w", P), ("value_w", P), ("query_w", P), ("blocks", P), ("key_b", 1))),
    ("attend", (("rep", HD * P), ("out_b", P), ("out_w_rep", HD * P), ("out_w", P))),
    ("routed", (("rank", OPS), ("logits", OPS), ("noise", OPS), ("ffn_w", OPS * P), ("ffn_b", OPS * P))),
    ("metric", (("ident", P), ("proj", P), ("proj_t", P), ("metric", P), ("mixer_w", P), ("mixer_b", P))),
    ("mlp", (("w1", HID), ("w2", HID), ("s1", NH), ("s2", NH), ("h1s", NH), ("h2s", NH), ("s3", P))),
    ("hidden1", (("h1", NH * HID),)),
    ("hidden2", (("h2", NH * HID), ("w3", NH * P))),
)


def first(group):
    return isinstance(group, int) and group == 0


def build(nc, x_tok, x_chan, packs, out):
    with ExitStack() as ctx:
        def sb(name, shape, dt=F32):
            return ctx.enter_context(nc.sbuf_tensor(name, shape, dt))

        def bank(name):
            return ctx.enter_context(nc.psum_tensor(name, [P, T], F32))

        def sem(name):
            return ctx.enter_context(nc.semaphore(name))

        pack_sb, view = {}, {}
        for pack, parts in PACKS:
            pack_sb[pack] = sb(pack + "_pack", [P, sum(n for _, n in parts)])
            at = 0
            for name, n in parts:
                view[name] = pack_sb[pack][:, at:at + n]
                at += n

        def cut(name, n):
            return view[name].rearrange("p (k c) -> p k c", k=n)

        key_w_sb, value_w_sb, query_w_sb, key_b_sb = view["key_w"], view["value_w"], view["query_w"], view["key_b"]
        rep_sb, blocks_sb, ident_sb = cut("rep", HD), view["blocks"], view["ident"]
        out_w_sb, out_w_rep_sb, out_b_sb = view["out_w"], cut("out_w_rep", HD), view["out_b"]
        rank_sb, logits_sb, noise_sb = view["rank"], view["logits"], view["noise"]
        ffn_w_sb, ffn_b_sb = cut("ffn_w", OPS), cut("ffn_b", OPS)
        proj_sb, proj_t_sb, metric_sb = view["proj"], view["proj_t"], view["metric"]
        mixer_w_sb, mixer_b_sb = view["mixer_w"], view["mixer_b"]
        w1_sb, w2_sb, h1_sb, h2_sb, w3_sb = view["w1"], view["w2"], cut("h1", NH), cut("h2", NH), cut("w3", NH)
        s1_sb, s2_sb, h1s_sb, h2s_sb, s3_sb = view["s1"], view["s2"], view["h1s"], view["h2s"], view["s3"]
        power = sb("power", [P, NT])
        route = sb("route", [P, 16, OPS])
        chosen_w, chosen_b = sb("chosen_w", [P, P]), sb("chosen_b", [P, P])
        proj_metric = sb("proj_metric", [P, P])
        xT, xt = sb("xT", [P, T]), sb("xt", [P, T])
        res0 = sb("res0", [P, T])
        keep = sb("keep", [P, T])
        query = sb("query", [P, T])
        value = sb("value", [P, GS, SEQ + 1])
        dvalue = sb("dvalue", [P, T])
        state = sb("state", [P, STATES, T])
        read = sb("read", [P, HD, T])
        direct = sb("direct", [P, T])
        total = [sb(f"total{n}", [P, T]) for n in range(4)]
        stats = [sb(f"stats{n}", [P, NT, 6]) for n in range(4)]
        moments = [sb(f"moments{n}", [P, NT, 2]) for n in range(4)]
        varied = [sb(f"varied{n}", [P, NT]) for n in range(4)]
        rstd = [sb(f"rstd{n}", [P, NT]) for n in range(4)]
        normed = [sb(f"normed{n}", [P, T]) for n in range(4)]
        x1T, x2T, x3T = sb("x1T", [P, T]), sb("x2T", [P, T]), sb("x3T", [P, T])
        res1, res2, res3 = sb("res1", [P, T]), sb("res2", [P, T]), sb("res3", [P, T])
        heads, moved = sb("heads", [P, T]), sb("moved", [P, T])
        gram, mixed = sb("gram", [P, GS, P]), sb("mixed", [P, GS, P])
        gate = sb("gate", [P, NH, T])
        hid = [sb(f"hid{n}", [P, NH, T]) for n in range(3)]
        scaled = sb("scaled", [P, T])

        rep_bank = [bank("rep_bank0"), bank("rep_bank1")]
        y1_bank, pj_bank = bank("y1_bank"), bank("pj_bank")
        b4_bank, b5_bank = bank("b4_bank"), bank("b5_bank")
        c_bank = [bank("c6_bank"), bank("c7_bank")]

        loaded = {pack: sem(pack + "_loaded") for pack, _ in PACKS}
        xT_loaded, xt_loaded, stored = sem("xT_loaded"), sem("xt_loaded"), sem("stored")
        const_ready, route_step, chosen_ready, pm_ready, pm_copied = (
            sem("const_ready"), sem("route_step"), sem("chosen_ready"), sem("pm_ready"), sem("pm_copied"))
        pj_ready, pj_free = sem("pj_ready"), sem("pj_free")
        dv_ready, rep_ready, scan_done, read_ready, y1_ready = (
            sem("dv_ready"), sem("rep_ready"), sem("scan_done"), sem("read_ready"), sem("y1_ready"))
        b_ready, b4_free, b5_free = sem("b_ready"), sem("b4_free"), sem("b5_free")
        c_ready = [sem("c6_ready"), sem("c7_ready")]
        c_free = [sem("c6_free"), sem("c7_free")]
        scaled_ready = sem("scaled_ready")
        res_ready = [sem(f"res{n}_ready") for n in range(4)]
        ln_sum = [sem(f"ln{n}_sum") for n in range(4)]
        ln_stats = [sem(f"ln{n}_stats") for n in range(4)]
        ln_moments = [sem(f"ln{n}_moments") for n in range(4)]
        ln_varied = [sem(f"ln{n}_varied") for n in range(4)]
        ln_rstd = [sem(f"ln{n}_rstd") for n in range(4)]
        ln_out = [sem(f"ln{n}_out") for n in range(4)]

        def tile(j):
            return slice(j * P, (j + 1) * P)

        def steps(step, eng):
            step(0, None, None)
            step(1, 0, None)
            with eng.Fori(0, NG - 2) as c:
                step(c + 2, c + 1, c)
            step(None, NG - 1, NG - 2)
            step(None, None, NG - 1)

        block = ctx.enter_context(nc.Block())

        @block.sync
        def _(sp):
            def load_pack(pack):
                sp.dma_start(pack_sb[pack][:], packs[pack]).then_inc(loaded[pack], 16)

            load_pack("project")

            def load(a):
                sp.dma_start(xT[:], x_chan[:, bass.ts(a, T)]).then_inc(xT_loaded, 16)
                sp.dma_start(xt[:].rearrange("p (j c) -> p j c", j=NT),
                             x_tok[bass.ts(a, NT), :, :].rearrange("j p c -> p j c")).then_inc(xt_loaded, 16)

            def step(a, b, c):
                if a is not None:
                    if not first(a):
                        sp.wait_ge(pj_ready, nth(a, PJ, -1))
                        sp.wait_ge(res_ready[0], a)
                    load(a)
                    if first(a):
                        for pack, _ in PACKS[1:]:
                            load_pack(pack)
                if c is not None:
                    sp.wait_ge(ln_out[3], nth(c, 1, 1))
                    sp.dma_start(out[bass.ts(c, NT), :, :].rearrange("j p c -> p j c"),
                                 normed[3][:].rearrange("p (j c) -> p j c", j=NT)).then_inc(stored, 16)

            steps(step, sp)
            sp.wait_ge(stored, 16 * NG)

        @block.gpsimd
        def _(pool):
            nc.gpsimd.memset(value[:], 0.0).then_inc(const_ready, 1)
            nc.gpsimd.memset(power[:], -0.5).then_inc(const_ready, 1)
            pool.wait_ge(const_ready, 2)

            def residual(n, group, out_, in_, bias):
                view = "p (j c) -> p j c"
                nc.gpsimd.tensor_tensor(out_[:].rearrange(view, j=NT), in_[:].rearrange(view, j=NT),
                                        bias[:].unsqueeze(1).to_broadcast([P, NT, P]), ALU.add).then_inc(res_ready[n], 1)

            def inverse_std(n, group):
                pool.wait_ge(ln_varied[n], nth(group, 1, 1))
                nc.gpsimd.tensor_tensor(rstd[n][:], varied[n][:], power[:], ALU.pow).then_inc(ln_rstd[n], 1)

            def step(a, b, c):
                if b is not None:
                    pool.wait_ge(ln_out[0], nth(b, 1, 1))
                    if first(b):
                        pool.wait_ge(chosen_ready, 2)
                    residual(1, b, res1, normed[0], chosen_b)
                if a is not None:
                    pool.wait_ge(xt_loaded, nth(a, 16, 16))
                    if first(a):
                        pool.wait_ge(loaded["attend"], 16)
                    residual(0, a, res0, xt, out_b_sb)
                if b is not None:
                    inverse_std(1, b)
                    pool.wait_ge(ln_out[1], nth(b, 1, 1))
                    if first(b):
                        pool.wait_ge(loaded["metric"], 16)
                    residual(2, b, res2, normed[1], mixer_b_sb)
                if a is not None:
                    inverse_std(0, a)
                if b is not None:
                    inverse_std(2, b)
                if c is not None:
                    inverse_std(3, c)

            steps(step, pool)

        @block.scalar
        def _(act):
            def routing():
                act.wait_ge(loaded["routed"], 16)
                act.wait_ge(route_step, 1)
                nc.scalar.activation(route[:, 1, :], route[:, 0, :], ACT.Exp, accum_out=route[:, 2, 0:1]).then_inc(route_step, 1)
                nc.scalar.activation(route[:, 3, :], noise_sb[:], ACT.Ln).then_inc(route_step, 1)
                act.wait_ge(route_step, 3)
                nc.scalar.activation(route[:, 4, 0:1], route[:, 2, 0:1], ACT.Ln).then_inc(route_step, 1)
                nc.scalar.activation(route[:, 5, :], route[:, 3, :], ACT.Ln, scale=-1.0).then_inc(route_step, 1)
                act.wait_ge(pm_ready, 1)
                nc.scalar.copy(proj_metric[:], b5_bank[:, 0:P]).then_inc(pm_copied, 1)

            def projection(a, k, out_, func, bias=0.0):
                act.wait_ge(pj_ready, nth(a, PJ, k))
                nc.scalar.activation(out_, pj_bank[:] if k != 2 else pj_bank[:].rearrange("p (s t) -> p s t", s=GS),
                                     func, bias=bias).then_inc(pj_free, 1)

            def move(b, k, out_, bank_, free, n=T):
                act.wait_ge(b_ready, nth(b, B4 + B5, k))
                nc.scalar.copy(out_, bank_[:, 0:n]).then_inc(free, 1)

            def silu(c, m):
                act.wait_ge(c_ready[0], nth(c, C6, m + 1))
                nc.scalar.activation(gate[:, m, :], c_bank[0][:], ACT.Silu, scale=s1_sb[:, m:m + 1]).then_inc(c_free[0], 1)

            def gelu(c, layer, m):
                per = (C6, C7)[m % 2]
                act.wait_ge(c_ready[m % 2], nth(c, per, NH + (layer - 1) * NH // 2 + m // 2 + 1))
                scale = (h1s_sb, h2s_sb)[layer - 1]
                nc.scalar.activation(hid[layer][:, m, :], c_bank[m % 2][:], ACT.Gelu,
                                     scale=scale[:, m:m + 1]).then_inc(c_free[m % 2], 1)

            def step(a, b, c):
                if b is not None:
                    move(b, 1, x1T[:], b4_bank, b4_free)
                if c is not None:
                    act.wait_ge(ln_out[2], nth(c, 1, 1))
                    act.wait_ge(ln_sum[3], nth(c, 1, 0) + CREDIT)
                    nc.scalar.copy(res3[:], normed[2][:]).then_inc(res_ready[3], 1)
                if a is not None:
                    if first(a):
                        act.wait_ge(loaded["project"], 16)
                        act.wait_ge(const_ready, 2)
                    else:
                        act.wait_ge(scan_done, nth(a, RP, 0))
                    projection(a, 1, keep[:], ACT.Sigmoid, bias=key_b_sb[:, 0:1])
                    projection(a, 2, value[:, :, 1:SEQ + 1], ACT.Copy)
                if c is not None:
                    silu(c, 0)
                    silu(c, 1)
                if a is not None:
                    if not first(a):
                        act.wait_ge(read_ready, nth(a, RP, 0))
                    projection(a, 3, query[:], ACT.Copy)
                    if first(a):
                        routing()
                if c is not None:
                    silu(c, 2)
                    silu(c, 3)
                    gelu(c, 1, 0)
                if b is not None:
                    move(b, 3, x2T[:], b4_bank, b4_free)
                if c is not None:
                    gelu(c, 1, 1)
                if b is not None:
                    move(b, 4, heads[:], b5_bank, b5_free)
                    move(b, 5, moved[:], b4_bank, b4_free)
                if c is not None:
                    gelu(c, 1, 2)
                    gelu(c, 1, 3)
                if b is not None:
                    move(b, 7, mixed[:].rearrange("p s c -> p (s c)"), b4_bank, b4_free, GS * P)
                if c is not None:
                    for m in range(NH):
                        gelu(c, 2, m)
                if b is not None:
                    move(b, 9, x3T[:], b4_bank, b4_free)

            steps(step, act)

        @block.vector
        def _(dve):
            def routing():
                v = nc.vector
                done = [0]

                def link(ins, to):
                    ins.then_inc(route_step, 1)
                    dve.wait_ge(route_step, to)

                dve.wait_ge(loaded["routed"], 16)
                v.reduce_max(route[:, 6, 0:1], logits_sb[:], AX_X).then_inc(chosen_ready, 1)
                dve.wait_ge(chosen_ready, 1)
                v.tensor_scalar(route[:, 0, :], logits_sb[:], route[:, 6, 0:1], None, ALU.subtract).then_inc(route_step, 1)
                dve.wait_ge(route_step, 5)
                link(v.tensor_scalar(route[:, 7, :], route[:, 0, :], route[:, 4, 0:1], None, ALU.subtract), 6)
                link(v.tensor_tensor(route[:, 8, :], route[:, 7, :], route[:, 5, :], ALU.subtract), 7)
                link(v.reduce_max(route[:, 9, 0:1], route[:, 8, :], AX_X), 8)
                link(v.tensor_scalar(route[:, 10, :], route[:, 8, :], route[:, 9, 0:1], None, ALU.is_equal), 9)
                link(v.tensor_tensor(route[:, 11, :], route[:, 10, :], rank_sb[:], ALU.mult), 10)
                link(v.reduce_max(route[:, 12, 0:1], route[:, 11, :], AX_X), 11)
                link(v.tensor_scalar(route[:, 13, :], route[:, 11, :], route[:, 12, 0:1], None, ALU.is_equal), 12)
                at = 12
                for o in range(OPS):
                    for dst, src in ((chosen_w, ffn_w_sb), (chosen_b, ffn_b_sb)):
                        hot = route[:, 13, o:o + 1]
                        if o == 0:
                            ins = v.tensor_scalar(dst[:], src[:, o, :], hot, None, ALU.mult)
                        else:
                            ins = v.scalar_tensor_tensor(dst[:], src[:, o, :], hot, dst[:], ALU.mult, ALU.add)
                        ins.then_inc(route_step, 1)
                        at += 1
                    dve.wait_ge(route_step, at)
                v.memset(route[:, 14, :], 0.0).then_inc(chosen_ready, 1)

            def norm_stats(n, group, ready, value_, bank_, free):
                dve.wait_ge(ready, value_)
                dve.wait_ge(res_ready[n], nth(group, 1, 1))
                ins = nc.vector.tensor_tensor(total[n][:], bank_[:], (res0, res1, res2, res3)[n][:], ALU.add)
                ins.then_inc(ln_sum[n], 1)
                dve.wait_ge(ln_sum[n], nth(group, 1, 1))
                norm_moments(n, group)

            def norm_moments(n, group):
                for j in range(NT):
                    ins = nc.vector.bn_stats(stats[n][:, j, :], total[n][:, tile(j)])
                ins.then_inc(ln_stats[n], 1)
                dve.wait_ge(const_ready, 2)
                dve.wait_ge(ln_stats[n], nth(group, 1, 1))
                for j in range(NT):
                    ins = nc.vector.bn_aggr(moments[n][:, j, :], stats[n][:, j, :])
                ins.then_inc(ln_moments[n], 1)
                dve.wait_ge(ln_moments[n], nth(group, 1, 1))
                nc.vector.tensor_scalar(varied[n][:], moments[n][:, :, 1], EPS, None, ALU.add).then_inc(ln_varied[n], 1)

            def norm_out(n, group):
                dve.wait_ge(ln_rstd[n], nth(group, 1, 1))
                if n == 2 and not first(group):
                    dve.wait_ge(res_ready[3], group)
                for j in range(NT):
                    ins = nc.vector.tensor_scalar(normed[n][:, tile(j)], total[n][:, tile(j)], moments[n][:, j, 0:1],
                                                  rstd[n][:, j:j + 1], ALU.subtract, ALU.mult)
                ins.then_inc(ln_out[n], 1)

            def scan(a, e):
                dve.wait_ge(rep_ready, nth(a, RP, e + 1))
                if e == 0:
                    dve.wait_ge(pj_free, nth(a, PJ, 1))
                if not first(a) or e >= STATES:
                    dve.wait_ge(read_ready, nth(a, RP, e + 1 - STATES))
                for s in range(GS):
                    at = slice(s * SEQ, (s + 1) * SEQ)
                    ins = nc.vector.tensor_tensor_scan(state[:, e % STATES, at], rep_bank[e % 2][:, at], keep[:, at], 0.0,
                                                       ALU.add, ALU.mult)
                ins.then_inc(scan_done, 1)

            def read_state(a, e):
                dve.wait_ge(scan_done, nth(a, RP, e + 1))
                if e == 0:
                    dve.wait_ge(pj_free, nth(a, PJ, 3))
                nc.vector.tensor_tensor(read[:, e, :], state[:, e % STATES, :], query[:], ALU.mult).then_inc(read_ready, 1)

            def product(c, m):
                dve.wait_ge(c_ready[1], nth(c, C7, m + 1))
                dve.wait_ge(c_free[0], nth(c, C6, m + 1) + CREDIT)
                nc.vector.scalar_tensor_tensor(hid[0][:, m, :], c_bank[1][:], s2_sb[:, m:m + 1], gate[:, m, :],
                                               ALU.mult, ALU.mult).then_inc(c_free[1], 1)

            def step(a, b, c):
                if c is not None:
                    product(c, 0)
                if a is not None:
                    if first(a):
                        dve.wait_ge(const_ready, 2)
                    dve.wait_ge(pj_free, nth(a, PJ, 2))
                    nc.vector.tensor_tensor(dvalue[:].rearrange("p (s t) -> p s t", s=GS), value[:, :, 0:SEQ],
                                            value[:, :, 1:SEQ + 1], ALU.subtract).then_inc(dv_ready, 1)
                if c is not None:
                    product(c, 1)
                if b is not None:
                    norm_stats(1, b, b_ready, nth(b, B4 + B5, 2), b5_bank, b5_free)
                if c is not None:
                    product(c, 2)
                    product(c, 3)
                if a is not None:
                    dve.wait_ge(pj_ready, nth(a, PJ, 4))
                    nc.vector.tensor_tensor(direct[:].rearrange("p (s t) -> p s t", s=GS),
                                            pj_bank[:].rearrange("p (s t) -> p s t", s=GS),
                                            value[:, :, 1:SEQ + 1], ALU.mult).then_inc(pj_free, 1)
                    scan(a, 0)
                    scan(a, 1)
                    read_state(a, 0)
                if b is not None:
                    norm_out(1, b)
                if a is not None:
                    for e in range(2, 6):
                        scan(a, e)
                        read_state(a, e - 1)
                if b is not None:
                    dve.wait_ge(b_ready, nth(b, B4 + B5, 6))
                    nc.vector.tensor_tensor(gram[:], b5_bank[:, 0:GS * P].rearrange("p (s c) -> p s c", s=GS),
                                            blocks_sb[:].unsqueeze(1).to_broadcast([P, GS, P]),
                                            ALU.mult).then_inc(b5_free, 1)
                if a is not None:
                    for e in range(6, HD):
                        scan(a, e)
                        read_state(a, e - 1)
                    read_state(a, HD - 1)
                if first(a):
                    routing()
                if b is not None:
                    norm_stats(2, b, b_ready, nth(b, B4 + B5, 8), b5_bank, b5_free)
                if a is not None:
                    norm_stats(0, a, y1_ready, nth(a, 1, 1), y1_bank, None)
                if b is not None:
                    norm_out(2, b)
                if a is not None:
                    norm_out(0, a)
                if c is not None:
                    dve.wait_ge(c_ready[0], nth(c, C6, C6))
                    nc.vector.tensor_tensor(scaled[:].rearrange("p (j c) -> p j c", j=NT),
                                            c_bank[0][:].rearrange("p (j c) -> p j c", j=NT),
                                            s3_sb[:].unsqueeze(1).to_broadcast([P, NT, P]),
                                            ALU.mult).then_inc(c_free[0], 1)
                    dve.wait_ge(c_free[0], nth(c, C6, C6) + CREDIT)
                    dve.wait_ge(res_ready[3], nth(c, 1, 1))
                    nc.vector.tensor_tensor(total[3][:], scaled[:], res3[:], ALU.add).then_inc(ln_sum[3], 1)
                    dve.wait_ge(ln_sum[3], nth(c, 1, 1) + CREDIT)
                    norm_moments(3, c)
                    if not first(c):
                        dve.wait_ge(stored, nth(c, 16, 0))
                    norm_out(3, c)

            steps(step, dve)

        @block.tensor
        def _(pe):
            def proj_step(a, k, w, src):
                if not first(a) or k > 1:
                    pe.wait_ge(pj_free, nth(a, PJ, k - 1))
                nc.tensor.matmul(pj_bank[:], w[:], src[:], start=True, stop=True).then_inc(pj_ready, 1)

            def replicate(a, e):
                if e == 0:
                    pe.wait_ge(dv_ready, nth(a, 1, 1))
                if not first(a) or e >= 2:
                    pe.wait_ge(scan_done, nth(a, RP, e - 1))
                nc.tensor.matmul(rep_bank[e % 2][:], rep_sb[:, e, :], dvalue[:], start=True,
                                 stop=True).then_inc(rep_ready, 1)

            def attend(a, e):
                pe.wait_ge(read_ready, nth(a, RP, e + 1))
                if e == 0 and not first(a):
                    pe.wait_ge(ln_sum[0], a)
                for j in range(NT):
                    nc.tensor.matmul(y1_bank[:, tile(j)], read[:, e, tile(j)], out_w_rep_sb[:, e, :],
                                     start=(e == 0 and j == 0), stop=False, skip_group_check=True)

            def attend_direct(a):
                pe.wait_ge(pj_free, nth(a, PJ, 4))
                for j in range(NT):
                    ins = nc.tensor.matmul(y1_bank[:, tile(j)], direct[:, tile(j)], out_w_sb[:],
                                           start=False, stop=(j == NT - 1), skip_group_check=True)
                ins.then_inc(y1_ready, 1)

            def transposes(b, n):
                pe.wait_ge(ln_out[n], nth(b, 1, 1))
                for j in range(NT):
                    ins = nc.tensor.transpose(b4_bank[:, tile(j)], normed[n][:, tile(j)], ident_sb[:])
                ins.then_inc(b_ready, 1)

            def per_tile(bank_, src, w):
                for j in range(NT):
                    ins = nc.tensor.matmul(bank_[:, tile(j)], src[:, tile(j)], w(j), start=True, stop=True)
                return ins

            def swiglu(c, m):
                for i, w in ((0, w1_sb), (1, w2_sb)):
                    pe.wait_ge(c_free[i], nth(c, (C6, C7)[i], m) + CREDIT)
                    nc.tensor.matmul(c_bank[i][:], w[:, tile(m)], x3T[:], start=True, stop=True).then_inc(c_ready[i], 1)

            def hidden(c, layer, m):
                at = NH + (layer - 1) * NH // 2
                if m == 0:
                    if layer == 1:
                        pe.wait_ge(c_free[1], nth(c, C7, NH) + CREDIT)
                    else:
                        for i in range(2):
                            pe.wait_ge(c_free[i], nth(c, (C6, C7)[i], at) + CREDIT)
                pe.wait_ge(c_free[m % 2], nth(c, (C6, C7)[m % 2], at + m // 2) + CREDIT)
                w = (h1_sb, h2_sb)[layer - 1]
                for k in range(NH):
                    ins = nc.tensor.matmul(c_bank[m % 2][:], w[:, k, tile(m)], hid[layer - 1][:, k, :],
                                           start=(k == 0), stop=(k == NH - 1))
                ins.then_inc(c_ready[m % 2], 1)

            def narrow(c):
                pe.wait_ge(c_free[0], nth(c, C6, C6 - 1) + CREDIT)
                pe.wait_ge(c_free[1], nth(c, C7, C7) + CREDIT)
                for j in range(NT):
                    for k in range(NH):
                        ins = nc.tensor.matmul(c_bank[0][:, tile(j)], hid[2][:, k, tile(j)], w3_sb[:, k, :],
                                               start=(k == 0), stop=(k == NH - 1))
                ins.then_inc(c_ready[0], 1)

            def step(a, b, c):
                if a is not None:
                    if first(a):
                        pe.wait_ge(loaded["project"], 16)
                    pe.wait_ge(xT_loaded, nth(a, 16, 16))
                    proj_step(a, 1, key_w_sb, xT)
                if b is not None:
                    if not first(b):
                        pe.wait_ge(b4_free, nth(b, B4, 0))
                    transposes(b, 0)
                if a is not None:
                    proj_step(a, 2, value_w_sb, xT)
                if c is not None:
                    pe.wait_ge(b4_free, nth(c, B4, B4))
                    swiglu(c, 0)
                if b is not None:
                    if not first(b):
                        pe.wait_ge(ln_sum[2], nth(b, 1, 0))
                    pe.wait_ge(b4_free, nth(b, B4, 1))
                    per_tile(b5_bank, x1T, lambda j: chosen_w[:]).then_inc(b_ready, 1)
                if c is not None:
                    swiglu(c, 1)
                if a is not None:
                    proj_step(a, 3, query_w_sb, xT)
                if c is not None:
                    swiglu(c, 2)
                if a is not None:
                    proj_step(a, 4, blocks_sb, query)
                    if first(a):
                        pe.wait_ge(loaded["attend"], 16)
                    replicate(a, 0)
                    replicate(a, 1)
                if c is not None:
                    swiglu(c, 3)
                    hidden(c, 1, 0)
                if a is not None:
                    replicate(a, 2)
                    attend(a, 0)
                if b is not None:
                    transposes(b, 1)
                if c is not None:
                    hidden(c, 1, 1)
                if b is not None:
                    pe.wait_ge(b4_free, nth(b, B4, 2))
                    per_tile(b5_bank, x2T, lambda j: proj_sb[:]).then_inc(b_ready, 1)
                    nc.tensor.matmul(b4_bank[:], proj_metric[:], x2T[:], start=True, stop=True).then_inc(b_ready, 1)
                if a is not None:
                    replicate(a, 3)
                    attend(a, 1)
                if c is not None:
                    hidden(c, 1, 2)
                if a is not None:
                    replicate(a, 4)
                    attend(a, 2)
                if b is not None:
                    pe.wait_ge(b5_free, nth(b, B5 - 2, 1))
                    for s in range(GS):
                        for j in range(TPS):
                            at = tile(s * TPS + j)
                            ins = nc.tensor.matmul(b5_bank[:, tile(s)], heads[:, at], heads[:, at],
                                                   start=(j == 0), stop=(j == TPS - 1))
                    ins.then_inc(b_ready, 1)
                if c is not None:
                    hidden(c, 1, 3)
                if a is not None:
                    replicate(a, 5)
                    attend(a, 3)
                if b is not None:
                    pe.wait_ge(b4_free, nth(b, B4, 3))
                    pe.wait_ge(b5_free, nth(b, B5 - 2, 2))
                    for s in range(GS):
                        ins = nc.tensor.matmul(b4_bank[:, tile(s)], gram[:, s, :], mixer_w_sb[:], start=True, stop=True)
                    ins.then_inc(b_ready, 1)
                if a is not None:
                    replicate(a, 6)
                    attend(a, 4)
                if c is not None:
                    hidden(c, 2, 0)
                if b is not None:
                    pe.wait_ge(b4_free, nth(b, B4, 4))
                    per_tile(b5_bank, moved, lambda j: mixed[:, j // TPS, :]).then_inc(b_ready, 1)
                if a is not None:
                    replicate(a, 7)
                    attend(a, 5)
                if c is not None:
                    hidden(c, 2, 1)
                if a is not None:
                    attend(a, 6)
                    attend(a, 7)
                    attend_direct(a)
                if first(a):
                    pe.wait_ge(loaded["metric"], 16)
                    nc.tensor.matmul(b5_bank[:, 0:P], proj_t_sb[:], metric_sb[:], start=True,
                                     stop=True).then_inc(pm_ready, 1)
                    pe.wait_ge(pm_copied, 1)
                    pe.wait_ge(chosen_ready, 2)
                    for pack in ("mlp", "hidden1", "hidden2"):
                        pe.wait_ge(loaded[pack], 16)
                if c is not None:
                    hidden(c, 2, 2)
                    hidden(c, 2, 3)
                if b is not None:
                    transposes(b, 2)
                if c is not None:
                    narrow(c)

            for freed in (*c_free, ln_sum[3]):
                pe.sem_inc(freed, CREDIT)
            steps(step, pe)


def kernel(L0_attn_x, L0_attn_key_w, L0_attn_key_b, L0_attn_vq_w, L0_attn_out_w, L0_attn_out_b, L0_ffn_W, L0_ffn_b,
           L0_ffn_logits, L0_ffn_u, L1_attn_projection_1nck, L1_attn_halves, L1_attn_diagonals_nk, L1_attn_mixer_w,
           L1_attn_mixer_b, L1_ffn_w1_w, L1_ffn_w1_s, L1_ffn_w2_w, L1_ffn_w2_s, L1_ffn_h1_w, L1_ffn_h1_s, L1_ffn_h2_w,
           L1_ffn_h2_s, L1_ffn_w3_w, L1_ffn_w3_s):
    import numpy as np
    import concourse.bacc as bacc
    from concourse.bass_utils import run_bass_kernel_spmd

    def rows(v):
        return np.broadcast_to(np.asarray(v).reshape(1, -1), (P, np.asarray(v).size))

    def per_chunk(v):
        return np.asarray(v).reshape(NH, P).T

    def contracted(w):
        return np.asarray(w).T.reshape(NH, P, -1).transpose(1, 0, 2)

    x = np.asarray(L0_attn_x).reshape(-1, P)
    vq = np.asarray(L0_attn_vq_w)
    out_t = np.asarray(L0_attn_out_w).T
    out_rep = np.broadcast_to(out_t.reshape(HEADS, 1, HD, P), (HEADS, HD, HD, P)).reshape(P, HD, P)
    rep = np.zeros((HEADS, HD, HD, HEADS, HD), np.float32)
    for h in range(HEADS):
        for e in range(HD):
            rep[h, e, e, h, :] = 1.0
    blocks = np.kron(np.eye(HEADS, dtype=np.float32), np.ones((HD, HD), np.float32))
    metric = np.zeros((HEADS, HD, HEADS, HD), np.float32)
    upper, lower = np.triu_indices(HD, k=1)
    for h in range(HEADS):
        metric[h, upper, h, lower] = np.asarray(L1_attn_halves)[h]
        metric[h, lower, h, upper] = np.asarray(L1_attn_halves)[h]
        metric[h, np.arange(HD), h, np.arange(HD)] = np.asarray(L1_attn_diagonals_nk)[h]
    proj = np.asarray(L1_attn_projection_1nck)[0].transpose(1, 0, 2).reshape(P, P)
    parts = {
        "key_w": np.asarray(L0_attn_key_w).T,
        "key_b": np.asarray(L0_attn_key_b).reshape(P, 1),
        "value_w": vq[:P].T,
        "query_w": vq[P:].T,
        "out_w": out_t,
        "out_w_rep": out_rep,
        "out_b": rows(L0_attn_out_b),
        "rep": rep.reshape(P, HD, P),
        "blocks": blocks,
        "ident": np.eye(P, dtype=np.float32),
        "rank": rows(np.arange(OPS, 0, -1, dtype=np.float32)),
        "ffn_w": np.asarray(L0_ffn_W).transpose(1, 0, 2),
        "ffn_b": rows(L0_ffn_b).reshape(P, OPS, P),
        "logits": rows(L0_ffn_logits),
        "noise": rows(L0_ffn_u),
        "proj": proj,
        "proj_t": proj.T,
        "metric": metric.reshape(P, P),
        "mixer_w": np.asarray(L1_attn_mixer_w).T,
        "mixer_b": rows(L1_attn_mixer_b),
        "w1": np.asarray(L1_ffn_w1_w).T,
        "s1": per_chunk(L1_ffn_w1_s),
        "w2": np.asarray(L1_ffn_w2_w).T,
        "s2": per_chunk(L1_ffn_w2_s),
        "h1": contracted(L1_ffn_h1_w),
        "h1s": per_chunk(L1_ffn_h1_s),
        "h2": contracted(L1_ffn_h2_w),
        "h2s": per_chunk(L1_ffn_h2_s),
        "w3": contracted(L1_ffn_w3_w),
        "s3": rows(L1_ffn_w3_s),
    }
    arrays = {"x_tok": x.reshape(-1, P, P), "x_chan": x.T}
    for pack, names in PACKS:
        arrays[pack] = np.concatenate([np.asarray(parts[name]).reshape(P, n) for name, n in names], axis=1)
    arrays = {name: np.ascontiguousarray(a) for name, a in arrays.items()}
    nc = bacc.Bacc("TRN2", target_bir_lowering=False, num_devices=1)
    ins = {name: nc.dram_tensor(name, a.shape, mybir.dt.from_np(a.dtype), kind="ExternalInput").ap()
           for name, a in arrays.items()}
    out = nc.dram_tensor("out", arrays["x_tok"].shape, F32, kind="ExternalOutput").ap()
    build(nc, ins["x_tok"], ins["x_chan"], ins, out)
    result = run_bass_kernel_spmd(nc, [arrays], core_ids=[0])
    return result.results[0]["out"].reshape(SEQS, SEQ, P)
```

```python
from contextlib import ExitStack

import concourse.bass as bass
from concourse import mybir

F32 = mybir.dt.float32
F32R = mybir.dt.float32r
I32 = mybir.dt.int32
ALU = mybir.AluOpType
ACT = mybir.ActivationFunctionType
AX_X = mybir.AxisListType.X

P = 128
SEQS, SEQ = 8, 256
GS = 2
T = GS * SEQ
NT = T // P
NG = SEQS // GS
TPS = SEQ // P
HEADS, HD = 16, 8
OPS = 8
HID = 512
NH = HID // P
EPS = 1e-5
STATES = 4
READS = 4
CREDIT = 1

RP, B4, B5, CB, OB, LOW, LAST = HD, 5, 4, 3 * NH // 2 + 1, NH // 2, 2 * NH, 3
PROJECTIONS = 3


def nth(group, per_group, k):
    return group * per_group + k


PACKS = (
    ("project", (("key_w", P), ("value_w", P), ("query_w", P), ("blocks", P), ("key_b", 1))),
    ("attend", (("rep", HD * P), ("out_b", P), ("out_w_rep", HD * P), ("out_w", P))),
    ("routed", (("ffn_w", OPS * P), ("ffn_b", OPS * P))),
    ("metric", (("ident", P), ("proj", P), ("proj_t", P), ("metric", P), ("mixer_w", P), ("mixer_b", P))),
    ("scales", (("rank", OPS), ("logits", OPS), ("noise", OPS), ("s1", NH), ("s2", NH), ("h1s", NH), ("h2s", NH), ("s3", 1))),
    ("mlp", (("w1", HID), ("w2", HID), ("w3", NH * P))),
    ("hidden1", (("h1", NH * HID),)),
    ("hidden2", (("h2", NH * HID),)),
)


def first(group):
    return isinstance(group, int) and group == 0


MLP_PACKS = ("mlp", "hidden1", "hidden2")
MLP_COLUMNS = {"mlp": 2 * HID + NH * P, "hidden1": NH * HID, "hidden2": NH * HID}


def build(nc, x_tok, x_chan, packs, out):
    with ExitStack() as ctx:
        def sb(name, shape, dt=F32):
            return ctx.enter_context(nc.sbuf_tensor(name, shape, dt))

        def bank(name):
            return ctx.enter_context(nc.psum_tensor(name, [P, T], F32))

        def sem(name):
            return ctx.enter_context(nc.semaphore(name))

        lent = {pack: sb(pack + "_lent", [P, 4 * T]) for pack in ("routed", "xT")}
        pack_sb, view = {}, {}
        for pack, parts in PACKS:
            n = sum(n for _, n in parts)
            pack_sb[pack] = lent["routed"][:] if pack == "routed" else sb(pack + "_pack", [P, n])[:]
            at = 0
            for name, n in parts:
                view[name] = pack_sb[pack][:, at:at + n]
                at += n

        def cut(name, n):
            return view[name].rearrange("p (k c) -> p k c", k=n)

        key_w_sb, value_w_sb, query_w_sb, key_b_sb = view["key_w"], view["value_w"], view["query_w"], view["key_b"]
        rep_sb, blocks_sb, ident_sb = cut("rep", HD), view["blocks"], view["ident"]
        out_w_sb, out_w_rep_sb, out_b_sb = view["out_w"], cut("out_w_rep", HD), view["out_b"]
        rank_sb, logits_sb, noise_sb = view["rank"], view["logits"], view["noise"]
        ffn_w_sb, ffn_b_sb = cut("ffn_w", OPS), cut("ffn_b", OPS)
        proj_sb, proj_t_sb, metric_sb = view["proj"], view["proj_t"], view["metric"]
        mixer_w_sb, mixer_b_sb = view["mixer_w"], view["mixer_b"]
        part = {pack: [sb(f"{pack}_{which}", [P, n], F32R) for which in ("high", "low")]
                for pack, n in MLP_COLUMNS.items()}
        w1_parts = [part["mlp"][i][:, 0:HID] for i in range(2)]
        w2_parts = [part["mlp"][i][:, HID:2 * HID] for i in range(2)]
        w3_parts = [part["mlp"][i][:, 2 * HID:].rearrange("p (k c) -> p k c", k=NH) for i in range(2)]
        h_parts = [[part[pack][i][:].rearrange("p (k c) -> p k c", k=NH) for i in range(2)]
                   for pack in ("hidden1", "hidden2")]
        low_sums = sb("low_sums", [P, 4])
        ones, low_flag = sb("ones", [P, P]), sb("low_flag", [P, 1], I32)
        rep_r = sb("rep_r", [P, HD, P], F32R)
        s1_sb, s2_sb, h1s_sb, h2s_sb, s3_sb = view["s1"], view["s2"], view["h1s"], view["h2s"], view["s3"]
        power = sb("power", [P, NT])
        route = sb("route", [P, 16, OPS])
        weighed = [lent["routed"][:, n * OPS * P:(n + 1) * OPS * P] for n in range(2)]
        chosen_w, chosen_b = sb("chosen_w", [P, P]), sb("chosen_b", [P, P])
        proj_metric = sb("proj_metric", [P, P])
        xT, xt = lent["xT"], sb("xt", [P, T])
        res0 = sb("res0", [P, T])
        keep = sb("keep", [P, NG * T])
        query = sb("query", [P, NG * T])
        value = sb("value", [P, SEQS, SEQ + 1])
        dvalue = sb("dvalue", [P, T])
        dvalue_parts = [sb(f"dvalue_{which}", [P, T], F32R) for which in ("high", "low")]
        state = sb("state", [P, STATES, T])
        read = sb("read", [P, READS, T])
        direct = sb("direct", [P, T])
        routed_lent = [lent["routed"][:, n * T:(n + 1) * T] for n in range(4)]
        xT_lent = [lent["xT"][:, n * T:(n + 1) * T] for n in range(4)]
        total = [sb("total0", [P, T])[:], routed_lent[0], routed_lent[1], xT_lent[2]]
        stats = [sb(f"stats{n}", [P, NT, 6]) for n in range(4)]
        moments = [sb(f"moments{n}", [P, NT, 2]) for n in range(4)]
        varied = [sb(f"varied{n}", [P, NT]) for n in range(4)]
        rstd = [sb(f"rstd{n}", [P, NT]) for n in range(4)]
        normed = [sb("normed0", [P, T])[:], routed_lent[2], routed_lent[3], xT_lent[3]]
        x1T = sb("x1T", [P, T])
        x2T = x1T
        x3T_parts = [sb(f"x3T_{which}", [P, T], F32R) for which in ("high", "low")]
        res1, res2, res3 = sb("res1", [P, T]), sb("res2", [P, T]), sb("res3", [P, T])
        heads, moved = xT_lent[0], xT_lent[1]
        gram, mixed = sb("gram", [P, GS, P]), sb("mixed", [P, GS, P])
        hid = pack_sb["hidden1"][:].rearrange("p (k t) -> p k t", k=NH)
        gate = pack_sb["hidden2"][:].rearrange("p (k t) -> p k t", k=NH)
        even, odd = ([sb(f"hid_{n}_{which}", [P, NH, T], F32R) for which in ("high", "low")] for n in ("even", "odd"))
        hid_parts = [even, odd, even]
        narrowed = gate[:, 0, :]

        rep_bank = [bank("rep_bank0"), bank("rep_bank1")]
        y1_bank = bank("y1_bank")
        b4_bank, b5_bank = bank("b4_bank"), bank("b5_bank")
        proj_bank = [bank("proj_bank"), b4_bank]
        c_bank = [bank("c6_bank"), bank("c7_bank")]

        loaded = {pack: sem(pack + "_loaded") for pack, _ in PACKS}
        xT_loaded = [sem(f"xT{g}_loaded") for g in range(NG)]
        xt_loaded, stored = sem("xt_loaded"), sem("stored")
        const_ready, route_step, chosen_ready, pm_ready, pm_copied = (
            sem("const_ready"), sem("route_step"), sem("chosen_ready"), sem("pm_ready"), sem("pm_copied"))
        proj_ready, proj_out = sem("proj_ready"), sem("proj_out")
        sum_ready, direct_ready, attended = sem("sum_ready"), sem("direct_ready"), sem("attended")
        dv_ready, rep_ready, scan_done, read_ready, y1_ready = (
            sem("dv_ready"), sem("rep_ready"), sem("scan_done"), sem("read_ready"), sem("y1_ready"))
        b_ready, b4_free, b5_free = sem("b_ready"), sem("b4_free"), sem("b5_free")
        c_ready = [sem("c6_ready"), sem("c7_ready")]
        c_free = [sem("c6_free"), sem("c7_free")]
        o_ready = [sem("o0_ready"), sem("o1_ready")]
        o_free = [sem("o0_free"), sem("o1_free")]
        x3_high, high0_ready = sem("x3_high"), sem("high0_ready")
        low_ready, low_last = sem("low_ready"), sem("low_last")
        high_ready, low_cut, last_cut, low_summed, flag_ready = (
            sem("high_ready"), sem("low_cut"), sem("last_cut"), sem("low_summed"), sem("flag_ready"))
        dv_step, rep_cast = sem("dv_step"), sem("rep_cast")
        res_ready = [sem(f"res{n}_ready") for n in range(4)]
        ln_sum = [sem(f"ln{n}_sum") for n in range(4)]
        ln_stats = [sem(f"ln{n}_stats") for n in range(4)]
        ln_moments = [sem(f"ln{n}_moments") for n in range(4)]
        ln_varied = [sem(f"ln{n}_varied") for n in range(4)]
        ln_rstd = [sem(f"ln{n}_rstd") for n in range(4)]
        ln_out = [sem(f"ln{n}_out") for n in range(4)]

        def tile(j):
            return slice(j * P, (j + 1) * P)

        def steps(step, eng):
            step(0, None, None)
            step(1, 0, None)
            with eng.Fori(0, NG - 2) as c:
                step(c + 2, c + 1, c)
            step(None, NG - 1, NG - 2)
            step(None, None, NG - 1)

        block = ctx.enter_context(nc.Block())

        @block.sync
        def _(sp):
            def load_pack(pack):
                sp.dma_start(pack_sb[pack][:], packs[pack]).then_inc(loaded[pack], 16)

            def load_tokens(g):
                sp.dma_start(xt[:].rearrange("p (j c) -> p j c", j=NT),
                             x_tok[bass.ts(g, NT), :, :].rearrange("j p c -> p j c")).then_inc(xt_loaded, 16)

            load_pack("project")
            for g in range(NG):
                at = slice(g * T, (g + 1) * T)
                sp.dma_start(xT[:, at], x_chan[:, at]).then_inc(xT_loaded[g], 16)
                if g == 0:
                    load_pack("attend")
            load_tokens(0)
            for pack in ("scales", "routed", "mlp", "hidden1", "hidden2", "metric"):
                load_pack(pack)
            with sp.Fori(1, NG) as g:
                sp.wait_ge(res_ready[0], g)
                load_tokens(g)
            with sp.Fori(0, NG) as g:
                sp.wait_ge(ln_out[3], nth(g, 1, 1))
                sp.dma_start(out[bass.ts(g, NT), :, :].rearrange("j p c -> p j c"),
                             normed[3].rearrange("p (j c) -> p j c", j=NT)).then_inc(stored, 16)
            sp.wait_ge(stored, 16 * NG)

        @block.gpsimd
        def _(pool):
            nc.gpsimd.memset(value[:], 0.0).then_inc(const_ready, 1)
            nc.gpsimd.memset(power[:], -0.5).then_inc(const_ready, 1)
            nc.gpsimd.memset(ones[:], 1.0).then_inc(const_ready, 1)
            pool.wait_ge(const_ready, 3)

            def residual(n, group, out_, in_, bias):
                view = "p (j c) -> p j c"
                nc.gpsimd.tensor_tensor(out_[:].rearrange(view, j=NT), in_[:].rearrange(view, j=NT),
                                        bias[:].unsqueeze(1).to_broadcast([P, NT, P]), ALU.add).then_inc(res_ready[n], 1)

            def inverse_std(n, group):
                pool.wait_ge(ln_varied[n], nth(group, 1, 1))
                nc.gpsimd.tensor_tensor(rstd[n][:], varied[n][:], power[:], ALU.pow).then_inc(ln_rstd[n], 1)

            def cut_weights(i):
                pack = MLP_PACKS[i]
                pool.wait_ge(high_ready, i + 1)
                nc.gpsimd.tensor_tensor(part[pack][1][:], pack_sb[pack], part[pack][0][:].bitcast(F32),
                                        ALU.subtract).then_inc(low_cut, 1)

            def low_part(layer, m):
                nc.gpsimd.tensor_tensor(hid_parts[layer][1][:, m, :], hid[:, m, :],
                                        hid_parts[layer][0][:, m, :].bitcast(F32), ALU.subtract).then_inc(low_ready, 1)

            def low_gelu(c, layer, m):
                pool.wait_ge(c_free[m % 2], nth(c, CB, NH // 2 * layer + m // 2 + 1) + CREDIT)
                low_part(layer, m)

            def step(a, b, c):
                if b is not None:
                    pool.wait_ge(ln_out[0], nth(b, 1, 1))
                    if first(b):
                        pool.wait_ge(chosen_ready, 2)
                    residual(1, b, res1, normed[0], chosen_b)
                if c is not None:
                    for m in range(NH // 2):
                        pool.wait_ge(high0_ready, nth(c, 2, 1))
                        low_part(0, m)
                if a is not None:
                    pool.wait_ge(xt_loaded, nth(a, 16, 16))
                    if first(a):
                        pool.wait_ge(loaded["attend"], 16)
                    residual(0, a, res0, xt, out_b_sb)
                if b is not None:
                    inverse_std(1, b)
                    pool.wait_ge(ln_out[1], nth(b, 1, 1))
                    if first(b):
                        pool.wait_ge(loaded["metric"], 16)
                    residual(2, b, res2, normed[1], mixer_b_sb)
                if c is not None:
                    for m in range(NH - 1):
                        low_gelu(c, 1, m)
                    for m in range(NH - 2):
                        low_gelu(c, 2, m)
                if first(a):
                    cut_weights(0)
                    cut_weights(1)
                if b is not None:
                    inverse_std(2, b)
                if a is not None:
                    inverse_std(0, a)
                if c is not None:
                    low_gelu(c, 2, NH - 2)
                    inverse_std(3, c)

            steps(step, pool)

        @block.scalar
        def _(act):
            def routing():
                act.wait_ge(route_step, 1)
                nc.scalar.activation(route[:, 1, :], route[:, 0, :], ACT.Exp, accum_out=route[:, 2, 0:1]).then_inc(route_step, 1)
                nc.scalar.activation(route[:, 3, :], noise_sb[:], ACT.Ln).then_inc(route_step, 1)
                act.wait_ge(route_step, 3)
                nc.scalar.activation(route[:, 4, 0:1], route[:, 2, 0:1], ACT.Ln).then_inc(route_step, 1)
                nc.scalar.activation(route[:, 5, :], route[:, 3, :], ACT.Ln, scale=-1.0).then_inc(route_step, 1)

            def projections(first_group, end):
                for n in range(PROJECTIONS * first_group, PROJECTIONS * end):
                    g, k = divmod(n, PROJECTIONS)
                    bank_ = proj_bank[n % 2]
                    act.wait_ge(proj_ready, n + 1)
                    if k == 0:
                        ins = nc.scalar.activation(keep[:, g * T:(g + 1) * T], bank_[:], ACT.Sigmoid, bias=key_b_sb)
                    elif k == 1:
                        ins = nc.scalar.copy(value[:, g * GS:(g + 1) * GS, 1:SEQ + 1],
                                             bank_[:].rearrange("p (s t) -> p s t", s=GS))
                    else:
                        ins = nc.scalar.copy(query[:, g * T:(g + 1) * T], bank_[:])
                    ins.then_inc(proj_out, 1)
                    if n == 1:
                        act.wait_ge(loaded["attend"], 16)
                        nc.scalar.copy(rep_r[:], rep_sb).then_inc(rep_cast, 1)

            def move(b, k, out_, bank_, free, n=T):
                act.wait_ge(b_ready, nth(b, B4 + B5, k))
                nc.scalar.copy(out_, bank_[:, 0:n]).then_inc(free, 1)

            def silu(c, m):
                ready, free, bank_ = ((c_ready, c_free, c_bank), (o_ready, o_free, rep_bank))[m % 2]
                act.wait_ge(ready[0], nth(c, (CB, OB)[m % 2], m // 2 + 1))
                nc.scalar.activation(gate[:, m, :], bank_[0][:], ACT.Silu, scale=s1_sb[:, m:m + 1]).then_inc(free[0], 1)

            def high_product(c, half):
                act.wait_ge(c_free[1], nth(c, CB, half + 1) + CREDIT)
                act.wait_ge(o_free[1], nth(c, OB, half + 1) + CREDIT)
                at = slice(half * NH // 2, (half + 1) * NH // 2)
                nc.scalar.copy(hid_parts[0][0][:, at, :], hid[:, at, :]).then_inc(high0_ready, 1)

            def split_weights():
                for pack in MLP_PACKS:
                    act.wait_ge(loaded[pack], 16)
                    nc.scalar.copy(part[pack][0][:], pack_sb[pack]).then_inc(high_ready, 1)

            def sum_low_parts():
                for i, pack in enumerate(MLP_PACKS):
                    act.wait_ge(*((low_cut, i + 1) if i < 2 else (last_cut, 1)))
                    nc.scalar.activation(pack_sb[pack], part[pack][1][:].bitcast(F32), ACT.Abs,
                                         accum_out=low_sums[:, i:i + 1]).then_inc(low_summed, 1)

            def gelu(c, layer, m):
                act.wait_ge(c_ready[m % 2], nth(c, CB, NH // 2 * layer + m // 2 + 1))
                scale = (h1s_sb, h2s_sb)[layer - 1][:, m:m + 1]
                nc.scalar.activation(hid[:, m, :], c_bank[m % 2][:], ACT.Gelu, scale=scale)
                nc.scalar.activation(hid_parts[layer][0][:, m, :], c_bank[m % 2][:], ACT.Gelu,
                                     scale=scale).then_inc(c_free[m % 2], 1)

            def step(a, b, c):
                if first(a):
                    act.wait_ge(loaded["project"], 16)
                    act.wait_ge(const_ready, 3)
                    projections(0, 2)
                    act.wait_ge(loaded["scales"], 16)
                    routing()
                    split_weights()
                if b is not None:
                    move(b, 1, x1T[:], b4_bank, b4_free)
                if first(b):
                    act.wait_ge(pm_ready, 1)
                    nc.scalar.copy(proj_metric[:], proj_bank[0][:, 0:P]).then_inc(pm_copied, 1)
                    projections(2, NG)
                if c is not None:
                    for m in range(NH):
                        silu(c, m)
                    act.wait_ge(ln_out[2], nth(c, 1, 1))
                    act.wait_ge(c_free[1], nth(c, CB, 0) + CREDIT)
                    nc.scalar.copy(res3[:], normed[2]).then_inc(res_ready[3], 1)
                    for half in range(2):
                        high_product(c, half)
                    for m in range(NH - 1):
                        gelu(c, 1, m)
                if b is not None:
                    move(b, 3, x2T[:], b4_bank, b4_free)
                if c is not None:
                    gelu(c, 1, NH - 1)
                if b is not None:
                    move(b, 4, heads, b5_bank, b5_free)
                    move(b, 5, moved, b4_bank, b4_free)
                if c is not None:
                    gelu(c, 2, 0)
                if b is not None:
                    move(b, 7, mixed[:].rearrange("p s c -> p (s c)"), b4_bank, b4_free, GS * P)
                if first(b):
                    sum_low_parts()
                if c is not None:
                    for m in range(1, NH):
                        gelu(c, 2, m)
                if b is not None:
                    move(b, 9, x3T_parts[0][:], b4_bank, x3_high)
                if c is not None:
                    act.wait_ge(c_ready[0], nth(c, CB, CB))
                    nc.scalar.activation(narrowed, c_bank[0][:], ACT.Copy, scale=s3_sb[:, 0:1]).then_inc(c_free[0], 1)

            steps(step, act)

        @block.vector
        def _(dve):
            def routing():
                v = nc.vector
                done = [0]

                def link(ins, to):
                    ins.then_inc(route_step, 1)
                    dve.wait_ge(route_step, to)

                dve.wait_ge(loaded["scales"], 16)
                v.reduce_max(route[:, 6, 0:1], logits_sb[:], AX_X).then_inc(chosen_ready, 1)
                dve.wait_ge(chosen_ready, 1)
                v.tensor_scalar(route[:, 0, :], logits_sb[:], route[:, 6, 0:1], None, ALU.subtract).then_inc(route_step, 1)
                dve.wait_ge(route_step, 5)
                link(v.tensor_scalar(route[:, 7, :], route[:, 0, :], route[:, 4, 0:1], None, ALU.subtract), 6)
                link(v.tensor_tensor(route[:, 8, :], route[:, 7, :], route[:, 5, :], ALU.subtract), 7)
                link(v.reduce_max(route[:, 9, 0:1], route[:, 8, :], AX_X), 8)
                link(v.tensor_scalar(route[:, 10, :], route[:, 8, :], route[:, 9, 0:1], None, ALU.is_equal), 9)
                link(v.tensor_tensor(route[:, 11, :], route[:, 10, :], rank_sb[:], ALU.mult), 10)
                link(v.reduce_max(route[:, 12, 0:1], route[:, 11, :], AX_X), 11)
                link(v.tensor_scalar(route[:, 13, :], route[:, 11, :], route[:, 12, 0:1], None, ALU.is_equal), 12)
                dve.wait_ge(loaded["routed"], 16)
                hot = route[:, 13, :].unsqueeze(2).to_broadcast([P, OPS, P])
                for n, src in ((0, ffn_w_sb), (1, ffn_b_sb)):
                    v.tensor_tensor(weighed[n].rearrange("p (o c) -> p o c", o=OPS), src, hot,
                                    ALU.mult).then_inc(route_step, 1)
                dve.wait_ge(route_step, 14)
                for n, dst in ((0, chosen_w), (1, chosen_b)):
                    ins = v.reduce_sum(dst[:], weighed[n].rearrange("p (o c) -> p c o", o=OPS), AX_X)
                ins.then_inc(chosen_ready, 1)

            def low_parts_flag():
                dve.wait_ge(flag_ready, 1)
                nc.vector.reduce_max(route[:, 15, 0:1], proj_bank[0][:, P:P + len(MLP_PACKS)], AX_X).then_inc(flag_ready, 1)
                dve.wait_ge(flag_ready, 2)
                nc.vector.tensor_scalar(low_flag[:], route[:, 15, 0:1], 0.0, None, ALU.is_gt).then_inc(flag_ready, 1)

            def norm_stats(n, group, ready, value_, bank_, free):
                dve.wait_ge(ready, value_)
                dve.wait_ge(res_ready[n], nth(group, 1, 1))
                ins = nc.vector.tensor_tensor(total[n][:], bank_[:], (res0, res1, res2, res3)[n][:], ALU.add)
                ins.then_inc(ln_sum[n], 1)
                dve.wait_ge(ln_sum[n], nth(group, 1, 1))
                norm_moments(n, group)

            def norm_moments(n, group):
                for j in range(NT):
                    ins = nc.vector.bn_stats(stats[n][:, j, :], total[n][:, tile(j)])
                ins.then_inc(ln_stats[n], 1)
                dve.wait_ge(const_ready, 3)
                dve.wait_ge(ln_stats[n], nth(group, 1, 1))
                for j in range(NT):
                    ins = nc.vector.bn_aggr(moments[n][:, j, :], stats[n][:, j, :])
                ins.then_inc(ln_moments[n], 1)
                dve.wait_ge(ln_moments[n], nth(group, 1, 1))
                nc.vector.tensor_scalar(varied[n][:], moments[n][:, :, 1], EPS, None, ALU.add).then_inc(ln_varied[n], 1)

            def norm_out(n, group):
                dve.wait_ge(ln_rstd[n], nth(group, 1, 1))
                if n == 2 and not first(group):
                    dve.wait_ge(res_ready[3], group)
                for j in range(NT):
                    ins = nc.vector.tensor_scalar(normed[n][:, tile(j)], total[n][:, tile(j)], moments[n][:, j, 0:1],
                                                  rstd[n][:, j:j + 1], ALU.subtract, ALU.mult)
                ins.then_inc(ln_out[n], 1)

            def scan(a, e):
                dve.wait_ge(rep_ready, nth(a, RP, e + 1))
                if not first(a) or e >= STATES:
                    dve.wait_ge(read_ready, nth(a, RP, e + 1 - STATES))
                for s in range(GS):
                    at = slice(s * SEQ, (s + 1) * SEQ)
                    ins = nc.vector.tensor_tensor_scan(state[:, e % STATES, at], rep_bank[e % 2][:, at],
                                                       keep[:, bass.ds(a * T + s * SEQ, SEQ)], 0.0, ALU.add, ALU.mult)
                ins.then_inc(scan_done, 1)

            def read_state(a, e):
                dve.wait_ge(scan_done, nth(a, RP, e + 1))
                if not first(a) or e >= READS:
                    dve.wait_ge(attended, nth(a, RP, e + 1 - READS))
                nc.vector.tensor_tensor(read[:, e % READS, :], state[:, e % STATES, :], query[:, bass.ts(a, T)],
                                        ALU.mult).then_inc(read_ready, 1)

            def product(c, m):
                ready, free, bank_ = ((c_ready, c_free, c_bank), (o_ready, o_free, rep_bank))[m % 2]
                per = (CB, OB)[m % 2]
                dve.wait_ge(ready[1], nth(c, per, m // 2 + 1))
                dve.wait_ge(free[0], nth(c, per, m // 2 + 1) + CREDIT)
                nc.vector.scalar_tensor_tensor(hid[:, m, :], bank_[1][:], s2_sb[:, m:m + 1], gate[:, m, :],
                                               ALU.mult, ALU.mult).then_inc(free[1], 1)

            def low_last_gelu(c, layer):
                m = NH - 1
                dve.wait_ge(c_free[m % 2], nth(c, CB, NH // 2 * layer + m // 2 + 1) + CREDIT)
                nc.vector.tensor_tensor(hid_parts[layer][1][:, m, :], hid[:, m, :],
                                        hid_parts[layer][0][:, m, :].bitcast(F32), ALU.subtract).then_inc(low_last, 1)

            def step(a, b, c):
                if c is not None:
                    for m in range(NH):
                        product(c, m)
                if a is not None:
                    if first(a):
                        dve.wait_ge(const_ready, 3)
                        dve.wait_ge(proj_out, 2)
                    seqs = bass.ts(a, GS)
                    nc.vector.tensor_tensor(dvalue[:].rearrange("p (s t) -> p s t", s=GS), value[:, seqs, 0:SEQ],
                                            value[:, seqs, 1:SEQ + 1], ALU.subtract).then_inc(dv_step, 1)
                    dve.wait_ge(dv_step, nth(a, 2, 1))
                    nc.vector.tensor_copy(dvalue_parts[0][:], dvalue[:]).then_inc(dv_step, 1)
                    dve.wait_ge(dv_step, nth(a, 2, 2))
                    nc.vector.tensor_tensor(dvalue_parts[1][:], dvalue[:], dvalue_parts[0][:].bitcast(F32),
                                            ALU.subtract).then_inc(dv_ready, 1)
                if c is not None:
                    at = slice(NH // 2, NH)
                    dve.wait_ge(high0_ready, nth(c, 2, 2))
                    nc.vector.tensor_tensor(hid_parts[0][1][:, at, :], hid[:, at, :],
                                            hid_parts[0][0][:, at, :].bitcast(F32), ALU.subtract).then_inc(low_last, 1)
                if b is not None:
                    norm_stats(1, b, b_ready, nth(b, B4 + B5, 2), b5_bank, b5_free)
                if a is not None:
                    dve.wait_ge(sum_ready, nth(a, 1, 1))
                    if first(a):
                        dve.wait_ge(proj_out, 3)
                    nc.vector.tensor_tensor(direct[:].rearrange("p (s t) -> p s t", s=GS),
                                            proj_bank[0][:].rearrange("p (s t) -> p s t", s=GS),
                                            value[:, bass.ts(a, GS), 1:SEQ + 1], ALU.mult).then_inc(direct_ready, 1)
                    scan(a, 0)
                    scan(a, 1)
                    read_state(a, 0)
                if b is not None:
                    norm_out(1, b)
                if a is not None:
                    for e in range(2, 5):
                        scan(a, e)
                        read_state(a, e - 1)
                if c is not None:
                    low_last_gelu(c, 1)
                if a is not None:
                    scan(a, 5)
                    read_state(a, 4)
                if b is not None:
                    dve.wait_ge(b_ready, nth(b, B4 + B5, 6))
                    nc.vector.tensor_tensor(gram[:], b5_bank[:, 0:GS * P].rearrange("p (s c) -> p s c", s=GS),
                                            blocks_sb.unsqueeze(1).to_broadcast([P, GS, P]),
                                            ALU.mult).then_inc(b5_free, 1)
                if a is not None:
                    for e in range(6, HD):
                        scan(a, e)
                        read_state(a, e - 1)
                    read_state(a, HD - 1)
                if first(a):
                    routing()
                    dve.wait_ge(high_ready, 3)
                    nc.vector.tensor_tensor(part["hidden2"][1][:], pack_sb["hidden2"],
                                            part["hidden2"][0][:].bitcast(F32), ALU.subtract).then_inc(last_cut, 1)
                if b is not None:
                    norm_stats(2, b, b_ready, nth(b, B4 + B5, 8), b5_bank, b5_free)
                if a is not None:
                    norm_stats(0, a, y1_ready, nth(a, 1, 1), y1_bank, None)
                if b is not None:
                    norm_out(2, b)
                if a is not None:
                    norm_out(0, a)
                if first(b):
                    low_parts_flag()
                    dve.wait_ge(proj_out, PROJECTIONS * NG)
                if c is not None:
                    low_last_gelu(c, 2)
                if b is not None:
                    dve.wait_ge(x3_high, nth(b, 1, 1))
                    nc.vector.tensor_tensor(x3T_parts[1][:], b4_bank[:], x3T_parts[0][:].bitcast(F32),
                                            ALU.subtract).then_inc(b4_free, 1)
                if c is not None:
                    dve.wait_ge(c_ready[1], nth(c, CB, CB))
                    dve.wait_ge(res_ready[3], nth(c, 1, 1))
                    nc.vector.tensor_tensor(total[3], c_bank[1][:], res3[:], ALU.add).then_inc(c_free[1], 1)
                    dve.wait_ge(c_free[1], nth(c, CB, CB) + CREDIT)
                    norm_moments(3, c)
                    if not first(c):
                        dve.wait_ge(stored, 16 * c)
                    norm_out(3, c)

            steps(step, dve)

        @block.tensor
        def _(pe):
            def project(n):
                g, k = divmod(n, PROJECTIONS)
                if k == 0:
                    pe.wait_ge(xT_loaded[g], 16)
                if n >= 2:
                    pe.wait_ge(proj_out, n - 1)
                if n == 4:
                    pe.wait_ge(direct_ready, 1)
                if n == 2 * PROJECTIONS:
                    pe.wait_ge(direct_ready, 2)
                if n == 2 * PROJECTIONS + 1:
                    pe.wait_ge(b4_free, 1)
                nc.tensor.matmul(proj_bank[n % 2][:], (key_w_sb, value_w_sb, query_w_sb)[k],
                                 xT[:, g * T:(g + 1) * T], start=True, stop=True).then_inc(proj_ready, 1)

            def sum_query(a):
                if first(a):
                    pe.wait_ge(proj_out, 3)
                else:
                    pe.wait_ge(direct_ready, a)
                nc.tensor.matmul(proj_bank[0][:], blocks_sb, query[:, bass.ts(a, T)], start=True,
                                 stop=True).then_inc(sum_ready, 1)

            def replicate(a, e):
                if e == 0:
                    pe.wait_ge(dv_ready, nth(a, 1, 1))
                if not first(a) or e >= 2:
                    pe.wait_ge(scan_done, nth(a, RP, e - 1))
                nc.tensor.matmul(rep_bank[e % 2][:], rep_r[:, e, :], dvalue_parts[0][:], start=True, stop=False)
                nc.tensor.matmul(rep_bank[e % 2][:], rep_r[:, e, :], dvalue_parts[1][:], start=False,
                                 stop=True).then_inc(rep_ready, 1)

            def attend(a, e):
                pe.wait_ge(read_ready, nth(a, RP, e + 1))
                if e == 0 and not first(a):
                    pe.wait_ge(ln_sum[0], a)
                for j in range(NT):
                    ins = nc.tensor.matmul(y1_bank[:, tile(j)], read[:, e % READS, tile(j)], out_w_rep_sb[:, e, :],
                                           start=(e == 0 and j == 0), stop=False, skip_group_check=True)
                ins.then_inc(attended, 1)

            def attend_direct(a):
                pe.wait_ge(direct_ready, nth(a, 1, 1))
                for j in range(NT):
                    ins = nc.tensor.matmul(y1_bank[:, tile(j)], direct[:, tile(j)], out_w_sb[:],
                                           start=False, stop=(j == NT - 1), skip_group_check=True)
                ins.then_inc(y1_ready, 1)

            def transposes(b, n):
                pe.wait_ge(ln_out[n], nth(b, 1, 1))
                for j in range(NT):
                    ins = nc.tensor.transpose(b4_bank[:, tile(j)], normed[n][:, tile(j)], ident_sb[:])
                ins.then_inc(b_ready, 1)

            def per_tile(bank_, src, w):
                for j in range(NT):
                    ins = nc.tensor.matmul(bank_[:, tile(j)], src[:, tile(j)], w(j), start=True, stop=True)
                return ins

            def by_parts(bank_, weights, inputs, low_waits=()):
                last = len(weights[0]) - 1
                for k in range(last + 1):
                    nc.tensor.matmul(bank_[:], weights[0][k], inputs[0][k], start=(k == 0), stop=False)
                for ready, value_ in low_waits:
                    pe.wait_ge(ready, value_)
                with nc.tensor.If(has_low[0]):
                    for k in range(last + 1):
                        for i in range(2):
                            nc.tensor.matmul(bank_[:], weights[1][k], inputs[i][k], start=False, stop=False)
                for k in range(last + 1):
                    ins = nc.tensor.matmul(bank_[:], weights[0][k], inputs[1][k], start=False, stop=(k == last))
                return ins

            def swiglu(c, m, groups_done):
                ready, free, bank_ = ((c_ready, c_free, c_bank), (o_ready, o_free, rep_bank))[m % 2]
                if m == 1:
                    pe.wait_ge(scan_done, RP * groups_done)
                for i, w in ((0, w1_parts), (1, w2_parts)):
                    pe.wait_ge(free[i], nth(c, (CB, OB)[m % 2], m // 2) + CREDIT)
                    by_parts(bank_[i], [[w[n][:, tile(m)]] for n in range(2)],
                             [[x3T_parts[n][:]] for n in range(2)]).then_inc(ready[i], 1)

            def hidden(c, layer, m):
                waits = ()
                if m == 0:
                    if layer == 1:
                        pe.wait_ge(high0_ready, nth(c, 2, 2))
                        waits = ((low_ready, nth(c, LOW, 2)), (low_last, nth(c, LAST, 1)))
                    else:
                        for i in range(2):
                            pe.wait_ge(c_free[i], nth(c, CB, NH) + CREDIT)
                        waits = ((low_ready, nth(c, LOW, NH + 1)), (low_last, nth(c, LAST, 2)))
                pe.wait_ge(c_free[m % 2], nth(c, CB, NH // 2 * layer + m // 2) + CREDIT)
                by_parts(c_bank[m % 2], [[w[:, k, tile(m)] for k in range(NH)] for w in h_parts[layer - 1]],
                         [[x[:, k, :] for k in range(NH)] for x in hid_parts[layer - 1]],
                         waits).then_inc(c_ready[m % 2], 1)

            def narrow(c):
                for i in range(2):
                    pe.wait_ge(c_free[i], nth(c, CB, CB - 1) + CREDIT)
                by_parts(c_bank[0], [[w[:, k, :] for k in range(NH)] for w in w3_parts],
                         [[x[:, k, :] for k in range(NH)] for x in hid_parts[2]],
                         ((low_ready, nth(c, LOW, LOW)), (low_last, nth(c, LAST, 3)))).then_inc(c_ready[0], 1)

            def turn_back(c):
                pe.wait_ge(c_free[0], nth(c, CB, CB) + CREDIT)
                for j in range(NT):
                    ins = nc.tensor.transpose(c_bank[1][:, tile(j)], narrowed[:, tile(j)], ident_sb[:])
                ins.then_inc(c_ready[1], 1)

            def step(a, b, c):
                if first(a):
                    pe.wait_ge(loaded["project"], 16)
                    for n in range(PROJECTIONS):
                        project(n)
                if b is not None:
                    if first(b):
                        pe.wait_ge(loaded["metric"], 16)
                    else:
                        pe.wait_ge(b4_free, nth(b, B4, 0))
                    transposes(b, 0)
                if c is not None:
                    pe.wait_ge(b4_free, nth(c, B4, B4))
                    groups_done = NG if a is None else a
                    swiglu(c, 0, groups_done)
                    swiglu(c, 1, groups_done)
                if b is not None:
                    if first(b):
                        pe.wait_ge(chosen_ready, 2)
                    else:
                        pe.wait_ge(ln_sum[2], nth(b, 1, 0))
                    pe.wait_ge(b4_free, nth(b, B4, 1))
                    per_tile(b5_bank, x1T, lambda j: chosen_w[:]).then_inc(b_ready, 1)
                if c is not None:
                    swiglu(c, 2, groups_done)
                    swiglu(c, 3, groups_done)
                if a is not None:
                    sum_query(a)
                    if first(a):
                        pe.wait_ge(loaded["attend"], 16)
                        pe.wait_ge(rep_cast, 1)
                    for i in range(2):
                        if c is not None:
                            pe.wait_ge(o_free[i], nth(c, OB, OB) + CREDIT)
                        replicate(a, i)
                if first(b):
                    pe.wait_ge(direct_ready, 2)
                    nc.tensor.matmul(proj_bank[0][:, 0:P], proj_t_sb, metric_sb, start=True,
                                     stop=True).then_inc(pm_ready, 1)
                    pe.wait_ge(pm_copied, 1)
                    for n in range(2 * PROJECTIONS, 3 * PROJECTIONS):
                        project(n)
                if c is not None:
                    hidden(c, 1, 0)
                    hidden(c, 1, 1)
                    hidden(c, 1, 2)
                if a is not None:
                    if first(a):
                        project(3)
                    attend(a, 0)
                    replicate(a, 2)
                if first(b):
                    for n in range(3 * PROJECTIONS, 4 * PROJECTIONS):
                        project(n)
                    pe.wait_ge(proj_out, PROJECTIONS * NG)
                if b is not None:
                    transposes(b, 1)
                if c is not None:
                    hidden(c, 1, 3)
                if a is not None:
                    if first(a):
                        project(4)
                    attend(a, 1)
                    replicate(a, 3)
                if b is not None:
                    pe.wait_ge(b4_free, nth(b, B4, 2))
                    per_tile(b5_bank, x2T, lambda j: proj_sb).then_inc(b_ready, 1)
                    nc.tensor.matmul(b4_bank[:], proj_metric[:], x2T[:], start=True, stop=True).then_inc(b_ready, 1)
                if a is not None:
                    if first(a):
                        project(5)
                    attend(a, 2)
                    replicate(a, 4)
                    attend(a, 3)
                    replicate(a, 5)
                if b is not None:
                    pe.wait_ge(b5_free, nth(b, B5 - 2, 1))
                    for s in range(GS):
                        for j in range(TPS):
                            at = tile(s * TPS + j)
                            ins = nc.tensor.matmul(b5_bank[:, tile(s)], heads[:, at], heads[:, at],
                                                   start=(j == 0), stop=(j == TPS - 1))
                    ins.then_inc(b_ready, 1)
                if c is not None:
                    hidden(c, 2, 0)
                if a is not None:
                    attend(a, 4)
                    replicate(a, 6)
                if b is not None:
                    pe.wait_ge(b4_free, nth(b, B4, 3))
                    pe.wait_ge(b5_free, nth(b, B5 - 2, 2))
                    for s in range(GS):
                        ins = nc.tensor.matmul(b4_bank[:, tile(s)], gram[:, s, :], mixer_w_sb, start=True, stop=True)
                    ins.then_inc(b_ready, 1)
                if a is not None:
                    attend(a, 5)
                    replicate(a, 7)
                if c is not None:
                    hidden(c, 2, 1)
                if b is not None:
                    pe.wait_ge(b4_free, nth(b, B4, 4))
                    per_tile(b5_bank, moved, lambda j: mixed[:, j // TPS, :]).then_inc(b_ready, 1)
                if a is not None:
                    attend(a, 6)
                    attend(a, 7)
                    attend_direct(a)
                if first(b):
                    pe.wait_ge(low_summed, len(MLP_PACKS))
                    nc.tensor.matmul(proj_bank[0][:, P:P + len(MLP_PACKS)], ones[:], low_sums[:, 0:len(MLP_PACKS)],
                                     start=True, stop=True).then_inc(flag_ready, 1)
                    pe.wait_ge(flag_ready, 3)
                    has_low.append(nc.tensor.value_load(low_flag[0:1, 0:1], min_val=0, max_val=1))
                if c is not None:
                    hidden(c, 2, 2)
                    hidden(c, 2, 3)
                if b is not None:
                    transposes(b, 2)
                if c is not None:
                    narrow(c)
                    turn_back(c)

            has_low = []
            for freed in (*c_free, *o_free):
                pe.sem_inc(freed, CREDIT)
            steps(step, pe)


def kernel(L0_attn_x, L0_attn_key_w, L0_attn_key_b, L0_attn_vq_w, L0_attn_out_w, L0_attn_out_b, L0_ffn_W, L0_ffn_b,
           L0_ffn_logits, L0_ffn_u, L1_attn_projection_1nck, L1_attn_halves, L1_attn_diagonals_nk, L1_attn_mixer_w,
           L1_attn_mixer_b, L1_ffn_w1_w, L1_ffn_w1_s, L1_ffn_w2_w, L1_ffn_w2_s, L1_ffn_h1_w, L1_ffn_h1_s, L1_ffn_h2_w,
           L1_ffn_h2_s, L1_ffn_w3_w, L1_ffn_w3_s):
    import numpy as np
    import concourse.bacc as bacc
    from concourse.bass_utils import run_bass_kernel_spmd

    def rows(v):
        return np.broadcast_to(np.asarray(v).reshape(1, -1), (P, np.asarray(v).size))

    def per_chunk(v):
        return np.asarray(v).reshape(NH, P).T

    def contracted(w):
        return np.asarray(w).T.reshape(NH, P, -1).transpose(1, 0, 2)

    x = np.asarray(L0_attn_x).reshape(-1, P)
    vq = np.asarray(L0_attn_vq_w)
    out_t = np.asarray(L0_attn_out_w).T
    out_rep = np.broadcast_to(out_t.reshape(HEADS, 1, HD, P), (HEADS, HD, HD, P)).reshape(P, HD, P)
    rep = np.zeros((HEADS, HD, HD, HEADS, HD), np.float32)
    for h in range(HEADS):
        for e in range(HD):
            rep[h, e, e, h, :] = 1.0
    blocks = np.kron(np.eye(HEADS, dtype=np.float32), np.ones((HD, HD), np.float32))
    metric = np.zeros((HEADS, HD, HEADS, HD), np.float32)
    upper, lower = np.triu_indices(HD, k=1)
    for h in range(HEADS):
        metric[h, upper, h, lower] = np.asarray(L1_attn_halves)[h]
        metric[h, lower, h, upper] = np.asarray(L1_attn_halves)[h]
        metric[h, np.arange(HD), h, np.arange(HD)] = np.asarray(L1_attn_diagonals_nk)[h]
    proj = np.asarray(L1_attn_projection_1nck)[0].transpose(1, 0, 2).reshape(P, P)
    parts = {
        "key_w": np.asarray(L0_attn_key_w).T,
        "key_b": np.asarray(L0_attn_key_b).reshape(P, 1),
        "value_w": vq[:P].T,
        "query_w": vq[P:].T,
        "out_w": out_t,
        "out_w_rep": out_rep,
        "out_b": rows(L0_attn_out_b),
        "rep": rep.reshape(P, HD, P),
        "blocks": blocks,
        "ident": np.eye(P, dtype=np.float32),
        "rank": rows(np.arange(OPS, 0, -1, dtype=np.float32)),
        "ffn_w": np.asarray(L0_ffn_W).transpose(1, 0, 2),
        "ffn_b": rows(L0_ffn_b).reshape(P, OPS, P),
        "logits": rows(L0_ffn_logits),
        "noise": rows(L0_ffn_u),
        "proj": proj,
        "proj_t": proj.T,
        "metric": metric.reshape(P, P),
        "mixer_w": np.asarray(L1_attn_mixer_w).T,
        "mixer_b": rows(L1_attn_mixer_b),
        "w1": np.asarray(L1_ffn_w1_w).T,
        "s1": per_chunk(L1_ffn_w1_s),
        "w2": np.asarray(L1_ffn_w2_w).T,
        "s2": per_chunk(L1_ffn_w2_s),
        "h1": contracted(L1_ffn_h1_w),
        "h1s": per_chunk(L1_ffn_h1_s),
        "h2": contracted(L1_ffn_h2_w),
        "h2s": per_chunk(L1_ffn_h2_s),
        "w3": contracted(L1_ffn_w3_w),
        "s3": np.asarray(L1_ffn_w3_s),
    }
    arrays = {"x_tok": x.reshape(-1, P, P), "x_chan": x.T}
    for pack, names in PACKS:
        arrays[pack] = np.concatenate([np.asarray(parts[name]).reshape(P, n) for name, n in names], axis=1)
    arrays = {name: np.ascontiguousarray(a) for name, a in arrays.items()}
    nc = bacc.Bacc("TRN2", target_bir_lowering=False, num_devices=1)
    ins = {name: nc.dram_tensor(name, a.shape, mybir.dt.from_np(a.dtype), kind="ExternalInput").ap()
           for name, a in arrays.items()}
    out = nc.dram_tensor("out", arrays["x_tok"].shape, F32, kind="ExternalOutput").ap()
    build(nc, ins["x_tok"], ins["x_chan"], ins, out)
    result = run_bass_kernel_spmd(nc, [arrays], core_ids=[0])
    return result.results[0]["out"].reshape(SEQS, SEQ, P)
```

```python
from contextlib import ExitStack

import concourse.bass as bass
from concourse import mybir

F32 = mybir.dt.float32
F32R = mybir.dt.float32r
I32 = mybir.dt.int32
ALU = mybir.AluOpType
ACT = mybir.ActivationFunctionType
AX_X = mybir.AxisListType.X

P = 128
SEQS, SEQ = 8, 256
GS = 2
T = GS * SEQ
NT = T // P
NG = SEQS // GS
TPS = SEQ // P
HEADS, HD = 16, 8
OPS = 8
HID = 512
NH = HID // P
EPS = 1e-5
STATES = 4
READS = 4
WARM_UP = 8
CREDIT = 1

RP, B4, B5, LOW, LAST, HIGH0 = HD, 5, 4, 2 * NH - 1, NH + 1, NH
CB = (3 * NH // 2 + 1, 3 * NH // 2)
OB = (NH // 2, NH // 2)
HIGH = 2 * NH
EARLY_LOWS = 2
POOL_GELUS = ((1, range(NH - 1)), (2, range(NH - 2)))
PROJECTIONS = 3


def nth(group, per_group, k):
    return group * per_group + k


PACKS = (
    ("project", (("key_w", P), ("value_w", P), ("query_w", P), ("blocks", P), ("key_b", 1))),
    ("attend", (("rep", HD * P), ("out_b", P), ("out_w_rep", HD * P), ("out_w", P))),
    ("routed", (("ffn_w", OPS * P), ("ffn_b", OPS * P))),
    ("metric", (("ident", P), ("proj", P), ("proj_t", P), ("metric", P), ("mixer_w", P), ("mixer_b", P))),
    ("scales", (("rank", OPS), ("logits", OPS), ("noise", OPS), ("s1", NH), ("s2", NH), ("h1s", NH), ("h2s", NH),
                ("s3", 1))),
    ("mlp", (("w1", HID), ("w2", HID), ("w3", NH * P))),
    ("hidden1", (("h1", NH * HID),)),
    ("hidden2", (("h2", NH * HID),)),
)


def first(group):
    return isinstance(group, int) and group == 0


MLP_PACKS = ("mlp", "hidden1", "hidden2")
MLP_COLUMNS = {"mlp": 2 * HID + NH * P, "hidden1": NH * HID, "hidden2": NH * HID}


def build(nc, x_tok, x_chan, packs, out):
    with ExitStack() as ctx:
        def sb(name, shape, dt=F32):
            return ctx.enter_context(nc.sbuf_tensor(name, shape, dt))

        def bank(name):
            return ctx.enter_context(nc.psum_tensor(name, [P, T], F32))

        def sem(name):
            return ctx.enter_context(nc.semaphore(name))

        lent = {pack: sb(pack + "_lent", [P, 4 * T]) for pack in ("routed", "xT")}
        pack_sb, view = {}, {}
        for pack, parts in PACKS:
            n = sum(n for _, n in parts)
            pack_sb[pack] = lent["routed"][:] if pack == "routed" else sb(pack + "_pack", [P, n])[:]
            at = 0
            for name, n in parts:
                view[name] = pack_sb[pack][:, at:at + n]
                at += n

        def cut(name, n):
            return view[name].rearrange("p (k c) -> p k c", k=n)

        key_w_sb, value_w_sb, query_w_sb, key_b_sb = view["key_w"], view["value_w"], view["query_w"], view["key_b"]
        rep_sb, blocks_sb, ident_sb = cut("rep", HD), view["blocks"], view["ident"]
        out_w_sb, out_w_rep_sb, out_b_sb = view["out_w"], cut("out_w_rep", HD), view["out_b"]
        rank_sb, logits_sb, noise_sb = view["rank"], view["logits"], view["noise"]
        ffn_w_sb, ffn_b_sb = cut("ffn_w", OPS), cut("ffn_b", OPS)
        proj_sb, proj_t_sb, metric_sb = view["proj"], view["proj_t"], view["metric"]
        mixer_w_sb, mixer_b_sb = view["mixer_w"], view["mixer_b"]
        part = {pack: [sb(f"{pack}_{which}", [P, n], F32R) for which in ("high", "low")]
                for pack, n in MLP_COLUMNS.items()}
        w1_parts = [part["mlp"][i][:, 0:HID] for i in range(2)]
        w2_parts = [part["mlp"][i][:, HID:2 * HID] for i in range(2)]
        w3_parts = [part["mlp"][i][:, 2 * HID:].rearrange("p (k c) -> p k c", k=NH) for i in range(2)]
        h_parts = [[part[pack][i][:].rearrange("p (k c) -> p k c", k=NH) for i in range(2)]
                   for pack in ("hidden1", "hidden2")]
        low_sums = sb("low_sums", [P, 4])
        ones, low_flag = sb("ones", [P, P]), sb("low_flag", [P, 1], I32)
        rep_r = sb("rep_r", [P, HD, P], F32R)
        s1_sb, s2_sb, h1s_sb, h2s_sb, s3_sb = view["s1"], view["s2"], view["h1s"], view["h2s"], view["s3"]
        power, spare = sb("power", [P, NT]), sb("spare", [P, 1])
        route = sb("route", [P, 16, OPS])
        weighed = [lent["routed"][:, n * OPS * P:(n + 1) * OPS * P] for n in range(2)]
        chosen_w, chosen_b = sb("chosen_w", [P, P]), sb("chosen_b", [P, P])
        proj_metric = sb("proj_metric", [P, P])
        xT, xt = lent["xT"], sb("xt", [P, T])
        res0 = sb("res0", [P, T])
        keep = sb("keep", [P, NG * T])
        query = sb("query", [P, NG * T])
        value = sb("value", [P, SEQS + GS, SEQ + 1])
        dvalue = sb("dvalue", [P, T])
        dvalue_parts = [sb(f"dvalue_{which}", [P, T], F32R) for which in ("high", "low")]
        state = sb("state", [P, STATES, T])
        read = sb("read", [P, READS, T])
        direct = sb("direct", [P, T])
        routed_lent = [lent["routed"][:, n * T:(n + 1) * T] for n in range(4)]
        xT_lent = [lent["xT"][:, n * T:(n + 1) * T] for n in range(4)]
        total = [sb("total0", [P, T])[:], routed_lent[0], routed_lent[1], xT_lent[2]]
        stats = [sb(f"stats{n}", [P, NT, 6]) for n in range(4)]
        moments = [sb(f"moments{n}", [P, NT, 2]) for n in range(4)]
        varied = [sb(f"varied{n}", [P, NT]) for n in range(4)]
        rstd = [sb(f"rstd{n}", [P, NT]) for n in range(4)]
        normed = [sb("normed0", [P, T])[:], routed_lent[2], routed_lent[3], xT_lent[3]]
        x1T = sb("x1T", [P, T])
        x2T = x1T
        x3T_parts = [sb(f"x3T_{which}", [P, T], F32R) for which in ("high", "low")]
        res1, res2, res3 = sb("res1", [P, T]), sb("res2", [P, T]), sb("res3", [P, T])
        heads, moved = xT_lent[0], xT_lent[1]
        gram, mixed = sb("gram", [P, GS, P]), sb("mixed", [P, GS, P])
        hid = pack_sb["hidden1"][:].rearrange("p (k t) -> p k t", k=NH)
        gate = pack_sb["hidden2"][:].rearrange("p (k t) -> p k t", k=NH)
        even, odd = ([sb(f"hid_{n}_{which}", [P, NH, T], F32R) for which in ("high", "low")] for n in ("even", "odd"))
        hid_parts = [even, odd, even]
        narrowed = gate[:, NH - 1, :]

        rep_bank = [bank("rep_bank0"), bank("rep_bank1")]
        y1_bank = bank("y1_bank")
        b4_bank, b5_bank = bank("b4_bank"), bank("b5_bank")
        proj_bank = [bank("proj_bank"), b4_bank]
        c_bank = [bank("c6_bank"), bank("c7_bank")]

        loaded = {pack: sem(pack + "_loaded") for pack, _ in PACKS}
        xT_loaded = [sem(f"xT{g}_loaded") for g in range(NG)]
        xt_loaded, stored = sem("xt_loaded"), sem("stored")
        const_ready, route_step, chosen_ready, pm_ready, pm_copied = (
            sem("const_ready"), sem("route_step"), sem("chosen_ready"), sem("pm_ready"), sem("pm_copied"))
        proj_ready, proj_out = sem("proj_ready"), sem("proj_out")
        sum_ready, direct_ready, attended = sem("sum_ready"), sem("direct_ready"), sem("attended")
        dv_ready, rep_ready, scan_done, read_ready, y1_ready = (
            sem("dv_ready"), sem("rep_ready"), sem("scan_done"), sem("read_ready"), sem("y1_ready"))
        b_ready, b4_free, b5_free = sem("b_ready"), sem("b4_free"), sem("b5_free")
        y1_summed = sem("y1_summed")
        c_ready = [sem("c6_ready"), sem("c7_ready")]
        c_free = [sem("c6_free"), sem("c7_free")]
        o_ready = [sem("o0_ready"), sem("o1_ready")]
        o_free = [sem("o0_free"), sem("o1_free")]
        x3_high, high0_ready, gelu_high = sem("x3_high"), sem("high0_ready"), sem("gelu_high")
        turned_ready = sem("turned_ready")
        low_ready, low_last = sem("low_ready"), sem("low_last")
        high_ready, low_cut, weighed_ready, low_summed, flag_ready = (
            sem("high_ready"), sem("low_cut"), sem("weighed_ready"), sem("low_summed"), sem("flag_ready"))
        dv_whole, dv_high = sem("dv_whole"), sem("dv_high")
        rep_cast = sem("rep_cast")
        res_ready = [sem(f"res{n}_ready") for n in range(4)]
        centred = sem("centred")
        ln_sum = {n: sem(f"ln{n}_sum") for n in (1, 2)}
        ln_stats = [sem(f"ln{n}_stats") for n in range(4)]
        ln_moments = [sem(f"ln{n}_moments") for n in range(4)]
        ln_varied = [sem(f"ln{n}_varied") for n in range(4)]
        ln_rstd = [sem(f"ln{n}_rstd") for n in range(4)]
        ln_out = [sem(f"ln{n}_out") for n in range(4)]

        def tile(j):
            return slice(j * P, (j + 1) * P)

        def y1_sums(a, c):
            return a if c is None else a + c

        def gated_banks(m):
            return ((o_ready, o_free, rep_bank, OB), (c_ready, c_free, c_bank, CB))[m % 2]

        def steps(step, eng):
            step(0, None, None)
            step(1, 0, None)
            with eng.Fori(0, NG - 2) as c:
                step(c + 2, c + 1, c)
            step(None, NG - 1, NG - 2)
            step(None, None, NG - 1)

        block = ctx.enter_context(nc.Block())

        @block.sync
        def _(sp):
            def load_pack(pack):
                sp.dma_start(pack_sb[pack][:], packs[pack]).then_inc(loaded[pack], 16)

            def load_tokens(g):
                sp.dma_start(xt[:].rearrange("p (j c) -> p j c", j=NT),
                             x_tok[bass.ts(g, NT), :, :].rearrange("j p c -> p j c")).then_inc(xt_loaded, 16)

            load_pack("project")
            for g in range(NG):
                at = slice(g * T, (g + 1) * T)
                sp.dma_start(xT[:, at], x_chan[:, at]).then_inc(xT_loaded[g], 16)
                if g == 0:
                    load_pack("scales")
                    load_pack("attend")
            load_tokens(0)
            for pack in ("routed", "mlp", "hidden1", "hidden2", "metric"):
                load_pack(pack)
            with sp.Fori(1, NG) as g:
                sp.wait_ge(res_ready[0], g)
                load_tokens(g)
            with sp.Fori(0, NG - 1) as g:
                sp.wait_ge(ln_out[3], nth(g, NT, NT))
                sp.dma_start(out[bass.ts(g, NT), :, :].rearrange("j p c -> p j c"),
                             normed[3].rearrange("p (j c) -> p j c", j=NT)).then_inc(stored, 16)
            sp.wait_ge(stored, 16 * (NG - 1 + CREDIT))
            for j in range(0, NT, NT // 2):
                sp.wait_ge(ln_out[3], nth(NG - 1, NT, j + NT // 2))
                sp.dma_start(out[(NG - 1) * NT + j:(NG - 1) * NT + j + NT // 2, :, :].rearrange("j p c -> p j c"),
                             normed[3][:, j * P:(j + NT // 2) * P].rearrange("p (j c) -> p j c", j=NT // 2)
                             ).then_inc(stored, 16)
            sp.wait_ge(stored, 16 * (NG + 1 + CREDIT))

        @block.gpsimd
        def _(pool):
            nc.gpsimd.memset(ones[:], 1.0).then_inc(const_ready, 1)
            nc.gpsimd.memset(value[:], 0.0).then_inc(const_ready, 1)
            nc.gpsimd.memset(power[:], -0.5).then_inc(const_ready, 1)
            pool.wait_ge(const_ready, 3)

            def residual(n, group, out_, in_, bias):
                view = "p (j c) -> p j c"
                nc.gpsimd.tensor_tensor(out_[:].rearrange(view, j=NT), in_[:].rearrange(view, j=NT),
                                        bias[:].unsqueeze(1).to_broadcast([P, NT, P]), ALU.add).then_inc(res_ready[n], 1)

            def inverse_std(n, group):
                pool.wait_ge(ln_varied[n], nth(group, 1, 1))
                nc.gpsimd.tensor_tensor(rstd[n][:], varied[n][:], power[:], ALU.pow).then_inc(ln_rstd[n], 1)

            def normalise_last(c):
                def tiles(x):
                    return x.rearrange("p (j c) -> p j c", j=NT)

                pool.wait_ge(stored, 16 * (c + CREDIT))
                nc.gpsimd.tensor_tensor(tiles(normed[3]), tiles(total[3]),
                                        moments[3][:, :, 0:1].to_broadcast([P, NT, P]), ALU.subtract).then_inc(centred, 1)
                pool.wait_ge(centred, nth(c, 1, 1))
                pool.wait_ge(ln_rstd[3], nth(c, 1, 1))
                nc.gpsimd.tensor_tensor(tiles(normed[3]), tiles(normed[3]),
                                        rstd[3][:].unsqueeze(2).to_broadcast([P, NT, P]), ALU.mult).then_inc(ln_out[3], NT)

            def weigh():
                pool.wait_ge(route_step, 12)
                pool.wait_ge(loaded["routed"], 16)
                hot = route[:, 13, :].unsqueeze(2).to_broadcast([P, OPS, P])
                for n, src in ((0, ffn_w_sb), (1, ffn_b_sb)):
                    nc.gpsimd.tensor_tensor(weighed[n].rearrange("p (o c) -> p o c", o=OPS), src, hot,
                                            ALU.mult).then_inc(weighed_ready, 1)

            def cut_weights(i):
                pack = MLP_PACKS[i]
                pool.wait_ge(high_ready, i + 1)
                nc.gpsimd.tensor_tensor(part[pack][1][:], pack_sb[pack], part[pack][0][:].bitcast(F32),
                                        ALU.subtract).then_inc(low_cut, 1)

            def low_part(layer, m):
                nc.gpsimd.tensor_tensor(hid_parts[layer][1][:, m, :], hid[:, m, :],
                                        hid_parts[layer][0][:, m, :].bitcast(F32), ALU.subtract).then_inc(low_ready, 1)

            def low_gelu(c, layer, m):
                pool.wait_ge(c_free[m % 2], nth(c, CB[m % 2], NH // 2 * layer + m // 2 + 1) + CREDIT)
                low_part(layer, m)

            def step(a, b, c):
                if a is not None:
                    pool.wait_ge(xt_loaded, nth(a, 16, 16))
                    if first(a):
                        pool.wait_ge(loaded["attend"], 16)
                    residual(0, a, res0, xt, out_b_sb)
                if first(b):
                    cut_weights(1)
                if b is not None:
                    inverse_std(1, b)
                    if first(b):
                        pool.wait_ge(loaded["metric"], 16)
                    if a is not None:
                        pool.wait_ge(ln_out[1], nth(b, NT, NT))
                        residual(2, b, res2, normed[1], mixer_b_sb)
                if c is not None:
                    for layer, chunks in POOL_GELUS:
                        for m in chunks:
                            low_gelu(c, layer, m)
                        if layer == 1 and a is None and b is not None:
                            pool.wait_ge(ln_out[1], nth(b, NT, NT))
                            residual(2, b, res2, normed[1], mixer_b_sb)
                if first(a):
                    weigh()
                    cut_weights(0)
                if first(b):
                    cut_weights(2)
                if b is not None:
                    inverse_std(2, b)
                if a is not None:
                    inverse_std(0, a)
                    pool.wait_ge(ln_out[0], nth(a, NT, NT))
                    if first(a):
                        pool.wait_ge(chosen_ready, 3)
                    residual(1, a, res1, normed[0], chosen_b)
                if b is not None:
                    for m in range(NH // 2):
                        pool.wait_ge(high0_ready, nth(b, HIGH0, m + 1))
                        low_part(0, m)
                if c is not None:
                    inverse_std(3, c)
                if a is not None and c is not None:
                    normalise_last(c)

            steps(step, pool)

        @block.scalar
        def _(act):
            def routing():
                act.wait_ge(route_step, 1)
                nc.scalar.activation(route[:, 1, :], route[:, 0, :], ACT.Exp, accum_out=route[:, 2, 0:1]).then_inc(route_step, 1)
                nc.scalar.activation(route[:, 3, :], noise_sb[:], ACT.Ln).then_inc(route_step, 1)
                act.wait_ge(route_step, 3)
                nc.scalar.activation(route[:, 4, 0:1], route[:, 2, 0:1], ACT.Ln).then_inc(route_step, 1)
                nc.scalar.activation(route[:, 5, :], route[:, 3, :], ACT.Ln, scale=-1.0).then_inc(route_step, 1)

            def projections(numbers):
                for n in numbers:
                    g, k = divmod(n, PROJECTIONS)
                    bank_ = proj_bank[n % 2]
                    act.wait_ge(proj_ready, n + 1)
                    if k == 0:
                        ins = nc.scalar.activation(keep[:, g * T:(g + 1) * T], bank_[:], ACT.Sigmoid, bias=key_b_sb)
                    elif k == 1:
                        ins = nc.scalar.copy(value[:, g * GS:(g + 1) * GS, 1:SEQ + 1],
                                             bank_[:].rearrange("p (s t) -> p s t", s=GS))
                    else:
                        ins = nc.scalar.copy(query[:, g * T:(g + 1) * T], bank_[:])
                    ins.then_inc(proj_out, 1)
                    if n == 1:
                        act.wait_ge(loaded["attend"], 16)
                        nc.scalar.copy(rep_r[:], rep_sb).then_inc(rep_cast, 1)

            def move(b, k, out_, bank_, free, n=T):
                act.wait_ge(b_ready, nth(b, B4 + B5, k))
                nc.scalar.copy(out_, bank_[:, 0:n]).then_inc(free, 1)

            def silu(c, m):
                ready, free, bank_, per = gated_banks(m)
                act.wait_ge(ready[0], nth(c, per[0], m // 2 + 1))
                nc.scalar.activation(gate[:, m, :], bank_[0][:], ACT.Silu, scale=s1_sb[:, m:m + 1]).then_inc(free[0], 1)

            def high_product(c, m):
                free, per = gated_banks(m)[1], gated_banks(m)[3]
                act.wait_ge(free[1], nth(c, per[1], m // 2 + 1) + CREDIT)
                nc.scalar.copy(hid_parts[0][0][:, m, :], hid[:, m, :]).then_inc(high0_ready, 1)

            def split_weights():
                for pack in MLP_PACKS:
                    act.wait_ge(loaded[pack], 16)
                    nc.scalar.copy(part[pack][0][:], pack_sb[pack]).then_inc(high_ready, 1)

            def sum_low_parts(packs_):
                for i in packs_:
                    pack = MLP_PACKS[i]
                    act.wait_ge(low_cut, i + 1)
                    nc.scalar.activation(pack_sb[pack], part[pack][1][:].bitcast(F32), ACT.Abs,
                                         accum_out=low_sums[:, i:i + 1]).then_inc(low_summed, 1)

            def gelu(c, layer, m):
                act.wait_ge(c_ready[m % 2], nth(c, CB[m % 2], NH // 2 * layer + m // 2 + 1))
                scale = (h1s_sb, h2s_sb)[layer - 1][:, m:m + 1]
                nc.scalar.activation(hid_parts[layer][0][:, m, :], c_bank[m % 2][:], ACT.Gelu,
                                     scale=scale).then_inc(gelu_high, 1)
                nc.scalar.activation(hid[:, m, :], c_bank[m % 2][:], ACT.Gelu, scale=scale).then_inc(c_free[m % 2], 1)

            def step(a, b, c):
                if first(a):
                    act.wait_ge(const_ready, 1)
                    nc.scalar.activation(spare[:], ones[:, 0:1], ACT.Sigmoid)
                    act.wait_ge(loaded["project"], 16)
                    act.wait_ge(const_ready, 3)
                    projections(range(0, PROJECTIONS))
                    act.wait_ge(loaded["scales"], 16)
                    routing()
                    split_weights()
                    projections(range(PROJECTIONS, 2 * PROJECTIONS))
                if first(b):
                    sum_low_parts((0,))
                    act.wait_ge(pm_ready, 1)
                    nc.scalar.copy(proj_metric[:], proj_bank[0][:, 0:P]).then_inc(pm_copied, 1)
                    projections(range(2 * PROJECTIONS, 3 * PROJECTIONS))
                    sum_low_parts((1,))
                if c is not None:
                    gelu(c, 1, 0)
                    act.wait_ge(ln_out[2], nth(c, NT, NT))
                    nc.scalar.copy(res3[:], normed[2]).then_inc(res_ready[3], 1)
                    for m in range(1, NH):
                        gelu(c, 1, m)
                if b is not None:
                    move(b, 3, x2T[:], b4_bank, b4_free)
                    move(b, 4, heads, b5_bank, b5_free)
                    move(b, 5, moved, b4_bank, b4_free)
                if first(b):
                    sum_low_parts((2,))
                if c is not None:
                    gelu(c, 2, 0)
                if b is not None:
                    move(b, 7, mixed[:].rearrange("p s c -> p (s c)"), b4_bank, b4_free, GS * P)
                if first(b):
                    projections(range(3 * PROJECTIONS, NG * PROJECTIONS - 1))
                if c is not None:
                    for m in range(1, NH):
                        gelu(c, 2, m)
                if b is not None:
                    move(b, 9, x3T_parts[0][:], b4_bank, x3_high)
                if b is not None and c is not None:
                    nc.scalar.activation(spare[:], ones[:, 0:1], ACT.Silu)
                if c is not None:
                    act.wait_ge(c_ready[0], nth(c, CB[0], CB[0]))
                    nc.scalar.activation(narrowed, c_bank[0][:], ACT.Copy, scale=s3_sb[:, 0:1]).then_inc(c_free[0], 1)
                if b is not None:
                    silu(b, 0)
                if first(b):
                    silu(b, 1)
                    high_product(b, 0)
                    projections((NG * PROJECTIONS - 1,))
                if a is not None:
                    move(a, 1, x1T[:], b4_bank, b4_free)
                if b is not None and not first(b):
                    silu(b, 1)
                    high_product(b, 0)
                if b is not None:
                    silu(b, 2)
                    high_product(b, 1)
                    silu(b, 3)
                    high_product(b, 2)
                    high_product(b, 3)

            steps(step, act)

        @block.vector
        def _(dve):
            def shifted_logits():
                v = nc.vector
                dve.wait_ge(loaded["scales"], 16)
                v.reduce_max(route[:, 6, 0:1], logits_sb[:], AX_X).then_inc(chosen_ready, 1)
                dve.wait_ge(chosen_ready, 1)
                v.tensor_scalar(route[:, 0, :], logits_sb[:], route[:, 6, 0:1], None, ALU.subtract).then_inc(route_step, 1)

            def route_on(k):
                v = nc.vector
                dve.wait_ge(route_step, 5 + k)
                if k == 0:
                    ins = v.tensor_scalar(route[:, 7, :], route[:, 0, :], route[:, 4, 0:1], None, ALU.subtract)
                elif k == 1:
                    ins = v.tensor_tensor(route[:, 8, :], route[:, 7, :], route[:, 5, :], ALU.subtract)
                elif k == 2:
                    ins = v.reduce_max(route[:, 9, 0:1], route[:, 8, :], AX_X)
                elif k == 3:
                    ins = v.tensor_scalar(route[:, 10, :], route[:, 8, :], route[:, 9, 0:1], None, ALU.is_equal)
                elif k == 4:
                    ins = v.tensor_tensor(route[:, 11, :], route[:, 10, :], rank_sb[:], ALU.mult)
                elif k == 5:
                    ins = v.reduce_max(route[:, 12, 0:1], route[:, 11, :], AX_X)
                else:
                    ins = v.tensor_scalar(route[:, 13, :], route[:, 11, :], route[:, 12, 0:1], None, ALU.is_equal)
                ins.then_inc(route_step, 1)

            def choose():
                for n, dst in ((0, chosen_w), (1, chosen_b)):
                    dve.wait_ge(weighed_ready, n + 1)
                    nc.vector.reduce_sum(dst[:], weighed[n].rearrange("p (o c) -> p c o", o=OPS),
                                         AX_X).then_inc(chosen_ready, 1)

            def low_parts_flag():
                dve.wait_ge(flag_ready, 1)
                nc.vector.reduce_max(route[:, 15, 0:1], proj_bank[0][:, P:P + len(MLP_PACKS)], AX_X).then_inc(flag_ready, 1)
                dve.wait_ge(flag_ready, 2)
                nc.vector.tensor_scalar(low_flag[:], route[:, 15, 0:1], 0.0, None, ALU.is_gt).then_inc(flag_ready, 1)

            def norm_sum(n, group, ready, value_, bank_, summed, sums):
                dve.wait_ge(ready, value_)
                dve.wait_ge(res_ready[n], nth(group, 1, 1))
                nc.vector.tensor_tensor(total[n][:], bank_[:], (res0, res1, res2, res3)[n][:],
                                        ALU.add).then_inc(summed, 1)
                dve.wait_ge(summed, sums)

            def norm_stats(n):
                for j in range(NT):
                    ins = nc.vector.bn_stats(stats[n][:, j, :], total[n][:, tile(j)])
                ins.then_inc(ln_stats[n], 1)

            def norm_aggregate(n, group):
                dve.wait_ge(const_ready, 3)
                dve.wait_ge(ln_stats[n], nth(group, 1, 1))
                for j in range(NT):
                    ins = nc.vector.bn_aggr(moments[n][:, j, :], stats[n][:, j, :])
                ins.then_inc(ln_moments[n], 1)
                dve.wait_ge(ln_moments[n], nth(group, 1, 1))
                nc.vector.tensor_scalar(varied[n][:], moments[n][:, :, 1], EPS, None, ALU.add).then_inc(ln_varied[n], 1)

            def norm_out(n, group):
                dve.wait_ge(ln_rstd[n], nth(group, 1, 1))
                if n == 2 and not first(group):
                    dve.wait_ge(res_ready[3], group)
                for j in range(NT):
                    nc.vector.tensor_scalar(normed[n][:, tile(j)], total[n][:, tile(j)], moments[n][:, j, 0:1],
                                            rstd[n][:, j:j + 1], ALU.subtract, ALU.mult).then_inc(ln_out[n], 1)

            def value_steps(a):
                seqs = bass.ts(a, GS)
                nc.vector.tensor_tensor(dvalue[:].rearrange("p (s t) -> p s t", s=GS), value[:, seqs, 0:SEQ],
                                        value[:, seqs, 1:SEQ + 1], ALU.subtract).then_inc(dv_whole, 1)

            def scan(a, e):
                dve.wait_ge(rep_ready, nth(a, RP, e + 1))
                if not first(a) or e >= STATES:
                    dve.wait_ge(read_ready, nth(a, RP, e + 1 - STATES))
                for s in range(GS):
                    at = slice(s * SEQ, (s + 1) * SEQ)
                    ins = nc.vector.tensor_tensor_scan(state[:, e % STATES, at], rep_bank[e % 2][:, at],
                                                       keep[:, bass.ds(a * T + s * SEQ, SEQ)], 0.0, ALU.add, ALU.mult)
                ins.then_inc(scan_done, 1)

            def read_state(a, e):
                dve.wait_ge(scan_done, nth(a, RP, e + 1))
                if not first(a) or e >= READS:
                    dve.wait_ge(attended, nth(a, RP, e + 1 - READS))
                nc.vector.tensor_tensor(read[:, e % READS, :], state[:, e % STATES, :], query[:, bass.ts(a, T)],
                                        ALU.mult).then_inc(read_ready, 1)

            def product(c, m):
                ready, free, bank_, per = gated_banks(m)
                dve.wait_ge(ready[1], nth(c, per[1], m // 2 + 1))
                dve.wait_ge(free[0], nth(c, per[0], m // 2 + 1) + CREDIT)
                nc.vector.scalar_tensor_tensor(hid[:, m, :], bank_[1][:], s2_sb[:, m:m + 1], gate[:, m, :],
                                               ALU.mult, ALU.mult).then_inc(free[1], 1)

            def low_last_gelu(c, layer, m):
                dve.wait_ge(c_free[m % 2], nth(c, CB[m % 2], NH // 2 * layer + m // 2 + 1) + CREDIT)
                nc.vector.tensor_tensor(hid_parts[layer][1][:, m, :], hid[:, m, :],
                                        hid_parts[layer][0][:, m, :].bitcast(F32), ALU.subtract).then_inc(low_last, 1)

            def low_x3T(b):
                dve.wait_ge(x3_high, nth(b, 1, 1))
                nc.vector.tensor_tensor(x3T_parts[1][:], b4_bank[:], x3T_parts[0][:].bitcast(F32),
                                        ALU.subtract).then_inc(b4_free, 1)

            def low_products(c):
                for m in range(NH // 2, NH):
                    dve.wait_ge(high0_ready, nth(c, HIGH0, m + 1))
                    nc.vector.tensor_tensor(hid_parts[0][1][:, m, :], hid[:, m, :],
                                            hid_parts[0][0][:, m, :].bitcast(F32), ALU.subtract).then_inc(low_last, 1)

            def step(a, b, c):
                if a is not None:
                    if first(a):
                        shifted_logits()
                        dve.wait_ge(const_ready, 3)
                        dve.wait_ge(proj_out, 2)
                    if first(b):
                        dve.wait_ge(proj_out, 2 * PROJECTIONS)
                    if first(a) or first(b):
                        value_steps(a)
                    dve.wait_ge(dv_whole, nth(a, 1, 1))
                    nc.vector.tensor_copy(dvalue_parts[0][:], dvalue[:]).then_inc(dv_high, 1)
                    dve.wait_ge(dv_high, nth(a, 1, 1))
                    nc.vector.tensor_tensor(dvalue_parts[1][:], dvalue[:], dvalue_parts[0][:].bitcast(F32),
                                            ALU.subtract).then_inc(dv_ready, 1)
                if a is not None:
                    dve.wait_ge(sum_ready, nth(a, 1, 1))
                    if first(a):
                        dve.wait_ge(proj_out, 3)
                    nc.vector.tensor_tensor(direct[:].rearrange("p (s t) -> p s t", s=GS),
                                            proj_bank[0][:].rearrange("p (s t) -> p s t", s=GS),
                                            value[:, bass.ts(a, GS), 1:SEQ + 1], ALU.mult).then_inc(direct_ready, 1)
                    scan(a, 0)
                    scan(a, 1)
                    read_state(a, 0)
                if b is not None:
                    norm_sum(1, b, b_ready, nth(b, B4 + B5, 2), b5_bank, ln_sum[1], nth(b, 1, 1))
                    norm_stats(1)
                    norm_aggregate(1, b)
                if a is not None:
                    if c is not None:
                        read_state(a, 1)
                    scan(a, 2)
                    if first(a):
                        route_on(0)
                    if c is None:
                        read_state(a, 1)
                    if first(a):
                        route_on(1)
                if b is not None:
                    norm_out(1, b)
                if a is not None:
                    for e in (3, 4):
                        if c is not None and e == 3:
                            read_state(a, e - 1)
                        scan(a, e)
                        if first(a):
                            route_on(2 * e - 4)
                        if not (c is not None and e == 3):
                            read_state(a, e - 1)
                        if first(a):
                            route_on(2 * e - 3)
                if c is not None:
                    low_last_gelu(c, 1, NH - 1)
                if first(b):
                    dve.wait_ge(proj_out, 3 * PROJECTIONS - 1)
                    value_steps(a + 1)
                if a is not None:
                    scan(a, 5)
                    if first(a):
                        route_on(6)
                    read_state(a, 4)
                if b is not None:
                    dve.wait_ge(b_ready, nth(b, B4 + B5, 6))
                    nc.vector.tensor_tensor(gram[:], b5_bank[:, 0:GS * P].rearrange("p (s c) -> p s c", s=GS),
                                            blocks_sb.unsqueeze(1).to_broadcast([P, GS, P]),
                                            ALU.mult).then_inc(b5_free, 1)
                if a is not None:
                    for e in range(6, HD):
                        scan(a, e)
                        read_state(a, e - 1)
                    read_state(a, HD - 1)
                if a is not None and c is not None:
                    value_steps(a + 1)
                if first(a):
                    choose()
                if first(b):
                    low_parts_flag()
                if b is not None:
                    norm_sum(2, b, b_ready, nth(b, B4 + B5, 8), b5_bank, ln_sum[2], nth(b, 1, 1))
                    norm_stats(2)
                    norm_aggregate(2, b)
                if first(b):
                    norm_out(2, b)
                    low_x3T(b)
                if a is not None:
                    norm_sum(0, a, y1_ready, nth(a, 1, 1), y1_bank, y1_summed, y1_sums(a, c) + 1)
                if b is not None and not first(b):
                    norm_out(2, b)
                if a is not None:
                    norm_stats(0)
                    norm_aggregate(0, a)
                if c is not None:
                    low_last_gelu(c, 2, NH - 2)
                    low_last_gelu(c, 2, NH - 1)
                if b is not None and not first(b):
                    low_x3T(b)
                if first(b):
                    product(b, 0)
                    product(b, 1)
                if a is not None:
                    norm_out(0, a)
                if first(b):
                    dve.wait_ge(proj_out, PROJECTIONS * NG)
                if b is not None and not first(b):
                    product(b, 0)
                if c is not None:
                    norm_sum(3, c, turned_ready, nth(c, 1, 1), y1_bank, y1_summed,
                             y1_sums(NG if a is None else a + 1, c) + 1)
                if b is not None and not first(b):
                    product(b, 1)
                if c is not None:
                    norm_stats(3)
                if b is not None:
                    product(b, 2)
                    product(b, 3)
                    low_products(b)
                if c is not None:
                    norm_aggregate(3, c)
                if a is None and c is not None:
                    dve.wait_ge(stored, 16 * (c + CREDIT))
                    norm_out(3, c)

            steps(step, dve)

        @block.tensor
        def _(pe):
            def project(n):
                g, k = divmod(n, PROJECTIONS)
                if k == 0:
                    pe.wait_ge(xT_loaded[g], 16)
                if n >= 2:
                    pe.wait_ge(proj_out, n - 1)
                if n == 4:
                    pe.wait_ge(direct_ready, 1)
                if n == 2 * PROJECTIONS:
                    pe.wait_ge(pm_copied, 1)
                if n == 2 * PROJECTIONS + 1:
                    pe.wait_ge(b4_free, 1)
                if n == 3 * PROJECTIONS:
                    pe.wait_ge(b4_free, B4 - 1)
                if n == 3 * PROJECTIONS + 2:
                    pe.wait_ge(b4_free, B4)
                if n == 3 * PROJECTIONS + 1:
                    pe.wait_ge(flag_ready, 2)
                nc.tensor.matmul(proj_bank[n % 2][:], (key_w_sb, value_w_sb, query_w_sb)[k],
                                 xT[:, g * T:(g + 1) * T], start=True, stop=True).then_inc(proj_ready, 1)

            def sum_query(a):
                if first(a):
                    pe.wait_ge(proj_out, 3)
                else:
                    pe.wait_ge(direct_ready, a)
                nc.tensor.matmul(proj_bank[0][:], blocks_sb, query[:, bass.ts(a, T)], start=True,
                                 stop=True).then_inc(sum_ready, 1)

            def replicate(a, e):
                if e == 0:
                    pe.wait_ge(dv_ready, nth(a, 1, 1))
                if not first(a) or e >= 2:
                    pe.wait_ge(scan_done, nth(a, RP, e - 1))
                nc.tensor.matmul(rep_bank[e % 2][:], rep_r[:, e, :], dvalue_parts[0][:], start=True, stop=False)
                nc.tensor.matmul(rep_bank[e % 2][:], rep_r[:, e, :], dvalue_parts[1][:], start=False,
                                 stop=True).then_inc(rep_ready, 1)

            def attend(a, c, e):
                pe.wait_ge(read_ready, nth(a, RP, e + 1))
                if e == 0 and not first(a):
                    pe.wait_ge(y1_summed, y1_sums(a, c))
                for j in range(NT):
                    ins = nc.tensor.matmul(y1_bank[:, tile(j)], read[:, e % READS, tile(j)], out_w_rep_sb[:, e, :],
                                           start=(e == 0 and j == 0), stop=False, skip_group_check=True)
                ins.then_inc(attended, 1)

            def attend_direct(a):
                pe.wait_ge(direct_ready, nth(a, 1, 1))
                for j in range(NT):
                    ins = nc.tensor.matmul(y1_bank[:, tile(j)], direct[:, tile(j)], out_w_sb[:],
                                           start=False, stop=(j == NT - 1), skip_group_check=True)
                ins.then_inc(y1_ready, 1)

            def transposes(b, n):
                for j in range(NT):
                    pe.wait_ge(ln_out[n], nth(b, NT, j + 1))
                    ins = nc.tensor.transpose(b4_bank[:, tile(j)], normed[n][:, tile(j)], ident_sb[:])
                ins.then_inc(b_ready, 1)

            def per_tile(bank_, src, w):
                for j in range(NT):
                    ins = nc.tensor.matmul(bank_[:, tile(j)], src[:, tile(j)], w(j), start=True, stop=True)
                return ins

            def by_parts(bank_, weights, inputs, ready=({}, {})):
                last = len(weights[0]) - 1

                def product_(k, i):
                    if k in ready[i]:
                        pe.wait_ge(*ready[i][k])
                    return nc.tensor.matmul(bank_[:], weights[0][k], inputs[i][k], start=(k == 0 and i == 0),
                                            stop=(k == last and i == 1))

                early = EARLY_LOWS if last in ready[0] and last > 0 else 0
                for k in range(last):
                    product_(k, 0)
                for k in range(early):
                    product_(k, 1)
                product_(last, 0)
                with nc.tensor.If(has_low[0]):
                    for k in range(last + 1):
                        if k in ready[1]:
                            pe.wait_ge(*ready[1][k])
                        for i in range(2):
                            nc.tensor.matmul(bank_[:], weights[1][k], inputs[i][k], start=False, stop=False)
                for k in range(early, last + 1):
                    ins = product_(k, 1)
                return ins

            def swiglu(c, m, groups_done):
                ready, free, bank_, per = gated_banks(m)
                if m == 0:
                    pe.wait_ge(scan_done, RP * groups_done)
                ready_parts = ({}, {})
                if m == 0:
                    ready_parts = ({0: (x3_high, nth(c, 1, 1))}, {0: (b4_free, nth(c, B4, B4))})
                for i, w in ((0, w1_parts), (1, w2_parts)):
                    pe.wait_ge(free[i], nth(c, per[i], m // 2) + CREDIT)
                    by_parts(bank_[i], [[w[n][:, tile(m)]] for n in range(2)],
                             [[x3T_parts[n][:]] for n in range(2)], ready_parts).then_inc(ready[i], 1)

            def gelus_ready(c, layer):
                high = {k: (gelu_high, nth(c, HIGH, NH * (layer - 1) + k + 1)) for k in range(NH)}
                chunks = POOL_GELUS[layer - 1][1]
                low = {k: (low_ready, nth(c, LOW, NH // 2 + (NH - 1) * (layer - 1) + k + 1)) for k in chunks}
                for k in range(len(chunks), NH):
                    low[k] = (low_last, nth(c, LAST, LAST - (0 if layer == 2 else 2) - (NH - 1 - k)))
                return high, low

            def hidden(c, layer, m):
                ready = ({}, {})
                if m == 0 and layer == 1:
                    ready = ({k: (high0_ready, nth(c, HIGH0, k + 1)) for k in range(NH)},
                             {k: (low_ready, nth(c, LOW, k + 1)) if k < NH // 2 else
                              (low_last, nth(c, LAST, k - NH // 2 + 1)) for k in range(NH)})
                if m == 0 and layer == 2:
                    ready = gelus_ready(c, 1)
                pe.wait_ge(c_free[m % 2], nth(c, CB[m % 2], NH // 2 * layer + m // 2) + CREDIT)
                by_parts(c_bank[m % 2], [[w[:, k, tile(m)] for k in range(NH)] for w in h_parts[layer - 1]],
                         [[x[:, k, :] for k in range(NH)] for x in hid_parts[layer - 1]],
                         ready).then_inc(c_ready[m % 2], 1)

            def narrow(c):
                pe.wait_ge(c_free[0], nth(c, CB[0], CB[0] - 1) + CREDIT)
                by_parts(c_bank[0], [[w[:, k, :] for k in range(NH)] for w in w3_parts],
                         [[x[:, k, :] for k in range(NH)] for x in hid_parts[2]],
                         gelus_ready(c, 2)).then_inc(c_ready[0], 1)

            def turn_back(a, c):
                pe.wait_ge(c_free[0], nth(c, CB[0], CB[0]) + CREDIT)
                pe.wait_ge(y1_summed, y1_sums(NG if a is None else a + 1, c))
                for j in range(NT):
                    ins = nc.tensor.transpose(y1_bank[:, tile(j)], narrowed[:, tile(j)], ident_sb[:])
                ins.then_inc(turned_ready, 1)

            def step(a, b, c):
                if first(a):
                    pe.wait_ge(loaded["project"], 16)
                    for n in range(PROJECTIONS):
                        project(n)
                if c is not None:
                    groups_done = NG if a is None else a
                    swiglu(c, 2, groups_done)
                    swiglu(c, 3, groups_done)
                if b is not None:
                    if first(b):
                        pe.wait_ge(chosen_ready, 3)
                    else:
                        pe.wait_ge(ln_sum[2], nth(b, 1, 0))
                    pe.wait_ge(b4_free, nth(b, B4, 1))
                    per_tile(b5_bank, x1T, lambda j: chosen_w[:]).then_inc(b_ready, 1)
                if a is not None:
                    if first(b):
                        pe.wait_ge(proj_out, 2 * PROJECTIONS)
                    sum_query(a)
                    if first(a):
                        pe.wait_ge(loaded["attend"], 16)
                        pe.wait_ge(rep_cast, 1)
                if c is not None:
                    hidden(c, 1, 0)
                    hidden(c, 1, 1)
                if a is not None:
                    for i in range(2):
                        if c is not None:
                            pe.wait_ge(o_free[i], nth(c, OB[i], OB[i]) + CREDIT)
                        replicate(a, i)
                if first(b):
                    pe.wait_ge(direct_ready, 2)
                    nc.tensor.matmul(proj_bank[0][:, 0:P], proj_t_sb, metric_sb, start=True,
                                     stop=True).then_inc(pm_ready, 1)
                    for n in range(2 * PROJECTIONS, 3 * PROJECTIONS):
                        project(n)
                if c is not None:
                    hidden(c, 1, 2)
                    hidden(c, 1, 3)
                if a is not None:
                    replicate(a, 2)
                    attend(a, c, 0)
                    replicate(a, 3)
                    attend(a, c, 1)
                if b is not None:
                    if first(b):
                        pe.wait_ge(proj_out, 3 * PROJECTIONS)
                    transposes(b, 1)
                if a is not None:
                    replicate(a, 4)
                    attend(a, c, 2)
                if a is None and b is not None:
                    hidden(c, 2, 0)
                if b is not None:
                    pe.wait_ge(b4_free, nth(b, B4, 2))
                    per_tile(b5_bank, x2T, lambda j: proj_sb).then_inc(b_ready, 1)
                    nc.tensor.matmul(b4_bank[:], proj_metric[:], x2T[:], start=True, stop=True).then_inc(b_ready, 1)
                if a is not None:
                    replicate(a, 5)
                    attend(a, c, 3)
                if c is not None:
                    if a is not None or b is None:
                        hidden(c, 2, 0)
                    else:
                        hidden(c, 2, 1)
                if b is not None:
                    pe.wait_ge(b5_free, nth(b, B5 - 2, 1))
                    for s in range(GS):
                        for j in range(TPS):
                            at = tile(s * TPS + j)
                            ins = nc.tensor.matmul(b5_bank[:, tile(s)], heads[:, at], heads[:, at],
                                                   start=(j == 0), stop=(j == TPS - 1))
                    ins.then_inc(b_ready, 1)
                if a is not None:
                    replicate(a, 6)
                    attend(a, c, 4)
                if b is not None:
                    pe.wait_ge(b4_free, nth(b, B4, 3))
                    pe.wait_ge(b5_free, nth(b, B5 - 2, 2))
                    for s in range(GS):
                        ins = nc.tensor.matmul(b4_bank[:, tile(s)], gram[:, s, :], mixer_w_sb, start=True, stop=True)
                    ins.then_inc(b_ready, 1)
                if a is not None:
                    replicate(a, 7)
                    attend(a, c, 5)
                if c is not None and (a is not None or b is None):
                    hidden(c, 2, 1)
                if first(b):
                    pe.wait_ge(low_summed, len(MLP_PACKS))
                    nc.tensor.matmul(proj_bank[0][:, P:P + len(MLP_PACKS)], ones[:], low_sums[:, 0:len(MLP_PACKS)],
                                     start=True, stop=True).then_inc(flag_ready, 1)
                if b is not None:
                    pe.wait_ge(b4_free, nth(b, B4, 4))
                    per_tile(b5_bank, moved, lambda j: mixed[:, j // TPS, :]).then_inc(b_ready, 1)
                if a is not None:
                    if first(b):
                        project(3 * PROJECTIONS)
                    attend(a, c, 6)
                    if first(b):
                        project(3 * PROJECTIONS + 1)
                    attend(a, c, 7)
                    attend_direct(a)
                if first(b):
                    pe.wait_ge(proj_out, PROJECTIONS * NG - 1)
                    pe.wait_ge(flag_ready, 3)
                    has_low.append(nc.tensor.value_load(low_flag[0:1, 0:1], min_val=0, max_val=1))
                if c is not None:
                    hidden(c, 2, 2)
                    hidden(c, 2, 3)
                if b is not None:
                    transposes(b, 2)
                if c is not None:
                    narrow(c)
                if c is not None and b is not None:
                    swiglu(b, 0, NG if a is None else a + 1)
                if first(b):
                    swiglu(b, 0, a + 1)
                    swiglu(b, 1, a + 1)
                    project(3 * PROJECTIONS + 2)
                    pe.wait_ge(proj_out, PROJECTIONS * NG)
                if a is not None:
                    if first(a):
                        for n in range(PROJECTIONS, 2 * PROJECTIONS):
                            project(n)
                        pe.wait_ge(loaded["metric"], 16)
                        pe.wait_ge(proj_out, 2 * PROJECTIONS)
                    if b is not None:
                        pe.wait_ge(b4_free, nth(b, B4, B4))
                    transposes(a, 0)
                if c is not None:
                    turn_back(a, c)
                if c is not None and b is not None:
                    swiglu(b, 1, NG if a is None else a + 1)

            has_low = []
            for freed in (*c_free, *o_free):
                pe.sem_inc(freed, CREDIT)
            pe.sem_inc(stored, 16 * CREDIT)
            pe.wait_ge(const_ready, 1)
            for _ in range(WARM_UP):
                nc.tensor.matmul(c_bank[0][:, 0:P], ones[:], ones[:], start=True, stop=True)
            steps(step, pe)


def kernel(L0_attn_x, L0_attn_key_w, L0_attn_key_b, L0_attn_vq_w, L0_attn_out_w, L0_attn_out_b, L0_ffn_W, L0_ffn_b,
           L0_ffn_logits, L0_ffn_u, L1_attn_projection_1nck, L1_attn_halves, L1_attn_diagonals_nk, L1_attn_mixer_w,
           L1_attn_mixer_b, L1_ffn_w1_w, L1_ffn_w1_s, L1_ffn_w2_w, L1_ffn_w2_s, L1_ffn_h1_w, L1_ffn_h1_s, L1_ffn_h2_w,
           L1_ffn_h2_s, L1_ffn_w3_w, L1_ffn_w3_s):
    import numpy as np
    import concourse.bacc as bacc
    from concourse.bass_utils import run_bass_kernel_spmd

    def rows(v):
        return np.broadcast_to(np.asarray(v).reshape(1, -1), (P, np.asarray(v).size))

    def per_chunk(v):
        return np.asarray(v).reshape(NH, P).T

    def contracted(w):
        return np.asarray(w).T.reshape(NH, P, -1).transpose(1, 0, 2)

    x = np.asarray(L0_attn_x).reshape(-1, P)
    vq = np.asarray(L0_attn_vq_w)
    out_t = np.asarray(L0_attn_out_w).T
    out_rep = np.broadcast_to(out_t.reshape(HEADS, 1, HD, P), (HEADS, HD, HD, P)).reshape(P, HD, P)
    rep = np.zeros((HEADS, HD, HD, HEADS, HD), np.float32)
    for h in range(HEADS):
        for e in range(HD):
            rep[h, e, e, h, :] = 1.0
    blocks = np.kron(np.eye(HEADS, dtype=np.float32), np.ones((HD, HD), np.float32))
    metric = np.zeros((HEADS, HD, HEADS, HD), np.float32)
    upper, lower = np.triu_indices(HD, k=1)
    for h in range(HEADS):
        metric[h, upper, h, lower] = np.asarray(L1_attn_halves)[h]
        metric[h, lower, h, upper] = np.asarray(L1_attn_halves)[h]
        metric[h, np.arange(HD), h, np.arange(HD)] = np.asarray(L1_attn_diagonals_nk)[h]
    proj = np.asarray(L1_attn_projection_1nck)[0].transpose(1, 0, 2).reshape(P, P)
    parts = {
        "key_w": np.asarray(L0_attn_key_w).T,
        "key_b": np.asarray(L0_attn_key_b).reshape(P, 1),
        "value_w": vq[:P].T,
        "query_w": vq[P:].T,
        "out_w": out_t,
        "out_w_rep": out_rep,
        "out_b": rows(L0_attn_out_b),
        "rep": rep.reshape(P, HD, P),
        "blocks": blocks,
        "ident": np.eye(P, dtype=np.float32),
        "rank": rows(np.arange(OPS, 0, -1, dtype=np.float32)),
        "ffn_w": np.asarray(L0_ffn_W).transpose(1, 0, 2),
        "ffn_b": rows(L0_ffn_b).reshape(P, OPS, P),
        "logits": rows(L0_ffn_logits),
        "noise": rows(L0_ffn_u),
        "proj": proj,
        "proj_t": proj.T,
        "metric": metric.reshape(P, P),
        "mixer_w": np.asarray(L1_attn_mixer_w).T,
        "mixer_b": rows(L1_attn_mixer_b),
        "w1": np.asarray(L1_ffn_w1_w).T,
        "s1": per_chunk(L1_ffn_w1_s),
        "w2": np.asarray(L1_ffn_w2_w).T,
        "s2": per_chunk(L1_ffn_w2_s),
        "h1": contracted(L1_ffn_h1_w),
        "h1s": per_chunk(L1_ffn_h1_s),
        "h2": contracted(L1_ffn_h2_w),
        "h2s": per_chunk(L1_ffn_h2_s),
        "w3": contracted(L1_ffn_w3_w),
        "s3": np.asarray(L1_ffn_w3_s),
    }
    arrays = {"x_tok": x.reshape(-1, P, P), "x_chan": x.T}
    for pack, names in PACKS:
        arrays[pack] = np.concatenate([np.asarray(parts[name]).reshape(P, n) for name, n in names], axis=1)
    arrays = {name: np.ascontiguousarray(a) for name, a in arrays.items()}
    nc = bacc.Bacc("TRN2", target_bir_lowering=False, num_devices=1)
    ins = {name: nc.dram_tensor(name, a.shape, mybir.dt.from_np(a.dtype), kind="ExternalInput").ap()
           for name, a in arrays.items()}
    out = nc.dram_tensor("out", arrays["x_tok"].shape, F32, kind="ExternalOutput").ap()
    build(nc, ins["x_tok"], ins["x_chan"], ins, out)
    result = run_bass_kernel_spmd(nc, [arrays], core_ids=[0])
    return result.results[0]["out"].reshape(SEQS, SEQ, P)
```
